# Optimizing a Trainium2 kernel written in Bass

```python
import numpy as np
import jax
import jax.numpy as jnp

def _softmax(x, axis=-1):
    return jax.nn.softmax(x, axis=axis)

def _gelu(x):
    return jax.nn.gelu(x, approximate=True)

def _silu(x):
    return jax.nn.silu(x)

def _sigmoid(x):
    return jax.nn.sigmoid(x)

def _layernorm(x, axis=-1, eps=1e-05):
    m = jnp.mean(x, axis=axis, keepdims=True)
    v = jnp.var(x, axis=axis, keepdims=True)
    return (x - m) / jnp.sqrt(v + eps)

def _scatter_add(tgt, idx, src, axis=0):
    return tgt.at[idx].add(src)

def _segment_sum(src, seg, n):
    return jax.ops.segment_sum(src, seg, n)
kernel_name = 'mk_adj_resnorm_d4_adj_r2_f8d417'

def setup_inputs(seed: int=0):
    np.random.seed(seed)
    _w = jnp.asarray

    def _rec_inputs():
        import jax
        import jax.numpy as jnp
        _gk = jax.random.key(seed)
        x = -0.0005207 + 1.001 * jax.random.normal(jax.random.fold_in(_gk, 1), (4096, 128), jnp.float32)
        _w = (1.0 + jnp.arange(4096, dtype=jnp.float32)) ** (-0.5)
        _w = _w / _w.mean()
        _pij = jnp.clip(0.000976562 * _w[:, None] * _w[None, :], 0.0, 1.0)
        _a = jax.random.uniform(jax.random.fold_in(_gk, 2), (4096, 4096)) < _pij
        _a = jnp.logical_or(_a, jnp.eye(4096, dtype=bool))
        _af = _a.astype(jnp.float32)
        _af = _af * jax.random.uniform(jax.random.fold_in(_gk, 3), (4096, 4096), jnp.float32, 0.05, 1)
        adj = _af
        return (x, adj)
    x, adj = _rec_inputs()

    def _L0_gnn_setup():
        import jax, jax.numpy as jnp
        import numpy as np
        N = 4096
        D = 128
        L = 3

        def _cxin_conv(x, a, eps, W, b):
            ax = a @ x
            h = ax + (1.0 + eps[0]) * ax
            for i in range(L):
                h = jax.nn.relu(h @ W[i].T + b[i])
            return h
        key = jax.random.key(seed)
        ks = jax.random.split(key, 8)
        s = 1.0 / np.sqrt(D)
        return {'x1': jax.random.normal(ks[0], (N, D), jnp.float32), 'x2': jax.random.normal(ks[1], (N, D), jnp.float32), 'G1': jax.random.uniform(ks[2], (N, N), jnp.float32), 'G2': jax.random.uniform(ks[3], (N, N), jnp.float32), 'eps1': jnp.zeros((1,), jnp.float32), 'eps2': jnp.zeros((1,), jnp.float32), 'W1': jax.random.normal(ks[4], (L, D, D), jnp.float32) * s, 'b1': jnp.zeros((L, D), jnp.float32), 'W2': jax.random.normal(ks[5], (L, D, D), jnp.float32) * s, 'b2': jnp.zeros((L, D), jnp.float32), 'Wm': jax.random.normal(ks[6], (D, 2 * D), jnp.float32) * (1.0 / np.sqrt(2 * D)), 'bm': jnp.zeros((D,), jnp.float32)}
    _L0_gnn_all = _L0_gnn_setup()
    _L0_gnn_in = {k: v for k, v in _L0_gnn_all.items() if k in ('x2', 'eps1', 'eps2', 'W1', 'b1', 'W2', 'b2', 'Wm', 'bm')}
    del _L0_gnn_all

    def _L1_gnn_setup():
        import jax, jax.numpy as jnp
        import numpy as np
        NEG_BIG = -9000000000000000.0
        ALPHA = 0.2
        key = jax.random.key(seed)
        k1, k2, k3, k4 = jax.random.split(key, 4)
        N, F_in, F_out = (4096, 128, 128)
        h = jax.random.normal(k1, (N, F_in), dtype=jnp.float32)
        adj = jax.random.randint(k2, (N, N), 0, 2).astype(jnp.float32)
        W = jax.random.normal(k3, (F_in, F_out), dtype=jnp.float32) * (1.414 / np.sqrt(F_in))
        a = jax.random.normal(k4, (2 * F_out, 1), dtype=jnp.float32) * (1.414 / np.sqrt(2 * F_out))
        return {'h': h, 'adj': adj, 'W': W, 'a': a}
    _L1_gnn_all = _L1_gnn_setup()
    _L1_gnn_in = {k: v for k, v in _L1_gnn_all.items() if k in ('W', 'a')}
    del _L1_gnn_all

    def _L2_gnn_setup():
        import jax, jax.numpy as jnp
        import numpy as np
        NEG_INF = -9000000000000000.0
        NEG_SLOPE = 0.2
        key = jax.random.key(seed)
        k1, k2, k3, k4 = jax.random.split(key, 4)
        N, d_in, d_out = (4096, 128, 128)
        x = jax.random.normal(k1, (N, d_in), dtype=jnp.float32)
        adj = jax.random.randint(k2, (N, N), 0, 2).astype(jnp.float32)
        W = jax.random.normal(k3, (d_in, d_out), dtype=jnp.float32) * (1.0 / np.sqrt(d_in))
        a = jax.random.normal(k4, (2 * d_out,), dtype=jnp.float32) * (1.0 / np.sqrt(2 * d_out))
        return {'x': x, 'adj': adj, 'W': W, 'a': a}
    _L2_gnn_all = _L2_gnn_setup()
    _L2_gnn_in = {k: v for k, v in _L2_gnn_all.items() if k in ('W', 'a')}
    del _L2_gnn_all

    def _L3_gnn_setup():
        import jax, jax.numpy as jnp
        import numpy as np
        MIN_NORM = 1e-15
        BALL_EPS = 1e-05
        C_IN = 1.0
        C_OUT = 1.0

        def _artanh(x):
            x = jnp.clip(x, -1.0 + 1e-07, 1.0 - 1e-07)
            return 0.5 * (jnp.log1p(x) - jnp.log1p(-x))

        def _norm(x):
            return jnp.maximum(jnp.linalg.norm(x, axis=-1, keepdims=True), MIN_NORM)

        def proj(x, c):
            norm = _norm(x)
            maxnorm = (1.0 - BALL_EPS) / jnp.sqrt(c)
            return jnp.where(norm > maxnorm, x / norm * maxnorm, x)

        def expmap0(u, c):
            sc = jnp.sqrt(c)
            un = _norm(u)
            return jnp.tanh(sc * un) * u / (sc * un)

        def logmap0(p, c):
            sc = jnp.sqrt(c)
            pn = _norm(p)
            return _artanh(sc * pn) * p / (sc * pn)

        def mobius_matvec(m, x, c):
            sc = jnp.sqrt(c)
            xn = _norm(x)
            mx = x @ m.T
            mxn = _norm(mx)
            res = jnp.tanh(mxn / xn * _artanh(sc * xn)) * mx / (mxn * sc)
            zero_row = jnp.all(mx == 0, axis=-1, keepdims=True)
            return jnp.where(zero_row, jnp.zeros((), dtype=res.dtype), res)

        def mobius_add(x, y, c):
            x2 = jnp.sum(x * x, axis=-1, keepdims=True)
            y2 = jnp.sum(y * y, axis=-1, keepdims=True)
            xy = jnp.sum(x * y, axis=-1, keepdims=True)
            num = (1.0 + 2.0 * c * xy + c * y2) * x + (1.0 - c * x2) * y
            denom = 1.0 + 2.0 * c * xy + c * c * x2 * y2
            return num / jnp.maximum(denom, MIN_NORM)
        key = jax.random.key(seed)
        k1, k2, k3, k4 = jax.random.split(key, 4)
        N, D_IN, D_OUT = (4096, 128, 128)
        x = proj(0.05 * jax.random.normal(k1, (N, D_IN), dtype=jnp.float32), C_IN)
        adj = jax.random.uniform(k2, (N, N), dtype=jnp.float32)
        adj = adj / jnp.sum(adj, axis=1, keepdims=True)
        bound = np.sqrt(2.0) * np.sqrt(6.0 / (D_IN + D_OUT))
        weight = jax.random.uniform(k3, (D_OUT, D_IN), dtype=jnp.float32, minval=-bound, maxval=bound)
        bias = 0.01 * jax.random.normal(k4, (D_OUT,), dtype=jnp.float32)
        return {'x': x, 'adj': adj, 'weight': weight, 'bias': bias}
    _L3_gnn_all = _L3_gnn_setup()
    _L3_gnn_in = {k: v for k, v in _L3_gnn_all.items() if k in ('weight', 'bias')}
    del _L3_gnn_all
    return {'x': x, 'adj': adj, 'L0_gnn_x2': _L0_gnn_in['x2'], 'L0_gnn_eps1': _L0_gnn_in['eps1'], 'L0_gnn_eps2': _L0_gnn_in['eps2'], 'L0_gnn_W1': _L0_gnn_in['W1'], 'L0_gnn_b1': _L0_gnn_in['b1'], 'L0_gnn_W2': _L0_gnn_in['W2'], 'L0_gnn_b2': _L0_gnn_in['b2'], 'L0_gnn_Wm': _L0_gnn_in['Wm'], 'L0_gnn_bm': _L0_gnn_in['bm'], 'L1_gnn_W': _L1_gnn_in['W'], 'L1_gnn_a': _L1_gnn_in['a'], 'L2_gnn_W': _L2_gnn_in['W'], 'L2_gnn_a': _L2_gnn_in['a'], 'L3_gnn_weight': _L3_gnn_in['weight'], 'L3_gnn_bias': _L3_gnn_in['bias']}

def reference(x, adj, L0_gnn_x2, L0_gnn_eps1, L0_gnn_eps2, L0_gnn_W1, L0_gnn_b1, L0_gnn_W2, L0_gnn_b2, L0_gnn_Wm, L0_gnn_bm, L1_gnn_W, L1_gnn_a, L2_gnn_W, L2_gnn_a, L3_gnn_weight, L3_gnn_bias):
    import jax
    import jax.numpy as jnp

    def _L0_gnn_ref(x1, x2, G1, G2, eps1, eps2, W1, b1, W2, b2, Wm, bm):
        import jax, jax.numpy as jnp
        import numpy as np
        N = 4096
        D = 128
        L = 3

        def _cxin_conv(x, a, eps, W, b):
            ax = a @ x
            h = ax + (1.0 + eps[0]) * ax
            for i in range(L):
                h = jax.nn.relu(h @ W[i].T + b[i])
            return h
        out1 = _cxin_conv(x1, G1, eps1, W1, b1)
        out2 = _cxin_conv(x2, G2, eps2, W2, b2)
        merged = jnp.concatenate((out1, out2), axis=1)
        return merged @ Wm.T + bm

    def _L1_gnn_ref(h, adj, W, a):
        import jax, jax.numpy as jnp
        import numpy as np
        NEG_BIG = -9000000000000000.0
        ALPHA = 0.2
        F_out = W.shape[1]
        Wh = h @ W
        a1 = a[:F_out, 0]
        a2 = a[F_out:, 0]
        s1 = Wh @ a1
        s2 = Wh @ a2
        e = jax.nn.leaky_relu(s1[:, None] + s2[None, :], negative_slope=ALPHA)
        e = jnp.where(adj > 0, e, NEG_BIG)
        attention = jax.nn.softmax(e, axis=1)
        h_prime = attention @ Wh
        return jax.nn.elu(h_prime)

    def _L2_gnn_ref(x, adj, W, a):
        import jax, jax.numpy as jnp
        import numpy as np
        NEG_INF = -9000000000000000.0
        NEG_SLOPE = 0.2
        d_out = W.shape[1]
        Wh = x @ W
        e_src = Wh @ a[:d_out]
        e_dst = Wh @ a[d_out:]
        e = jax.nn.leaky_relu(e_src[:, None] + e_dst[None, :], NEG_SLOPE)
        N = Wh.shape[0]
        mask = (adj > 0) | jnp.eye(N, dtype=bool)
        e = jnp.where(mask, e, NEG_INF)
        alpha = jax.nn.softmax(e, axis=1)
        h = alpha @ Wh
        return h

    def _L3_gnn_ref(x, adj, weight, bias):
        import jax, jax.numpy as jnp
        import numpy as np
        MIN_NORM = 1e-15
        BALL_EPS = 1e-05
        C_IN = 1.0
        C_OUT = 1.0

        def _artanh(x):
            x = jnp.clip(x, -1.0 + 1e-07, 1.0 - 1e-07)
            return 0.5 * (jnp.log1p(x) - jnp.log1p(-x))

        def _norm(x):
            return jnp.maximum(jnp.linalg.norm(x, axis=-1, keepdims=True), MIN_NORM)

        def proj(x, c):
            norm = _norm(x)
            maxnorm = (1.0 - BALL_EPS) / jnp.sqrt(c)
            return jnp.where(norm > maxnorm, x / norm * maxnorm, x)

        def expmap0(u, c):
            sc = jnp.sqrt(c)
            un = _norm(u)
            return jnp.tanh(sc * un) * u / (sc * un)

        def logmap0(p, c):
            sc = jnp.sqrt(c)
            pn = _norm(p)
            return _artanh(sc * pn) * p / (sc * pn)

        def mobius_matvec(m, x, c):
            sc = jnp.sqrt(c)
            xn = _norm(x)
            mx = x @ m.T
            mxn = _norm(mx)
            res = jnp.tanh(mxn / xn * _artanh(sc * xn)) * mx / (mxn * sc)
            zero_row = jnp.all(mx == 0, axis=-1, keepdims=True)
            return jnp.where(zero_row, jnp.zeros((), dtype=res.dtype), res)

        def mobius_add(x, y, c):
            x2 = jnp.sum(x * x, axis=-1, keepdims=True)
            y2 = jnp.sum(y * y, axis=-1, keepdims=True)
            xy = jnp.sum(x * y, axis=-1, keepdims=True)
            num = (1.0 + 2.0 * c * xy + c * y2) * x + (1.0 - c * x2) * y
            denom = 1.0 + 2.0 * c * xy + c * c * x2 * y2
            return num / jnp.maximum(denom, MIN_NORM)
        h = proj(mobius_matvec(weight, x, C_IN), C_IN)
        hyp_bias = proj(expmap0(bias[None, :], C_IN), C_IN)
        h = proj(mobius_add(h, hyp_bias, C_IN), C_IN)
        x_tangent = logmap0(h, C_IN)
        support_t = adj @ x_tangent
        h = proj(expmap0(support_t, C_IN), C_IN)
        xt = jax.nn.relu(logmap0(h, C_IN))
        return proj(expmap0(xt, C_OUT), C_OUT)
    x = _layernorm(x + _L0_gnn_ref(x, L0_gnn_x2, adj, adj, L0_gnn_eps1, L0_gnn_eps2, L0_gnn_W1, L0_gnn_b1, L0_gnn_W2, L0_gnn_b2, L0_gnn_Wm, L0_gnn_bm), axis=-1)
    x = _layernorm(x + _L1_gnn_ref(x, adj, L1_gnn_W, L1_gnn_a), axis=-1)
    x = _layernorm(x + _L2_gnn_ref(x, adj, L2_gnn_W, L2_gnn_a), axis=-1)
    x = _layernorm(x + _L3_gnn_ref(x, adj, L3_gnn_weight, L3_gnn_bias), axis=-1)
    return x

_drawn_inputs = setup_inputs


def setup_inputs(seed=0):
    import zlib

    import numpy as np

    out = dict(_drawn_inputs(seed))
    spreads = {'L0_gnn_b1': (0.0, 0.1), 'L0_gnn_b2': (0.0, 0.1), 'L0_gnn_bm': (0.0, 0.1)}
    factors = {}
    for name, (base, spread) in spreads.items():
        noise = np.random.default_rng([zlib.crc32(name.encode()), seed]).standard_normal(out[name].shape)
        drawn = base * np.exp(spread * noise) if base else spread * noise
        out[name] = jnp.asarray(drawn.astype(out[name].dtype))
    for name, factor in factors.items():
        out[name] = (out[name] * factor).astype(out[name].dtype)
    return out
```

```python
import concourse.bass as bass
from concourse import mybir
from concourse.alu_op_type import AluOpType as ALU
from contextlib import ExitStack
import math

F32 = mybir.dt.float32
F32R = mybir.dt.float32r
U8 = mybir.dt.uint8
ACT = mybir.ActivationFunctionType
AX = mybir.AxisListType

P = 128
D = 128
N = 4096
BLOCK = 1024
BLOCKS = N // BLOCK
TILES = N // P
SUB = BLOCK // P
STREAM = BLOCKS * TILES
HALF = 512
RING = 4
ROOTS = (1, 1, 3, 2)
LN_EPS = 1e-5
MIN_NORM = 1e-15
MAX_NORM = 1.0 - 1e-5
CLIP = 1.0 - 2.0 ** -23
ATANH_MAX = 0.5 * (math.log1p(MAX_NORM) - math.log1p(-MAX_NORM))


class Chain:

    def __init__(self, eng, sem, per=0):
        self.eng, self.sem, self.per, self.n, self.blk = eng, sem, per, 0, 0

    def block(self, blk):
        self.blk, self.n = blk, 0

    def step(self, ins):
        ins.then_inc(self.sem, 1)
        self.n += 1
        self.eng.wait_ge(self.sem, self.blk * self.per + self.n)

    def end(self):
        assert self.n == self.per, (self.n, self.per)


def pipelined(eng, stream, epilogue, chain=None):
    for jt in range(TILES):
        stream(0, jt)
    with eng.Fori(1, BLOCKS) as blk:
        if chain:
            chain.block(blk - 1)
        for jt in range(TILES):
            stream(blk, jt)
            epilogue(blk - 1, jt)
        if chain:
            chain.end()
    if chain:
        chain.block(BLOCKS - 1)
    for step in range(TILES):
        epilogue(BLOCKS - 1, step)


def build(nc, adj, x, x2, wmlp, bmlp, eps, bm, gw, gwt, glast, ga, hwt, hw, hbias, hbcol, ident_in, out):
    ctx = ExitStack()
    with ctx:
        def sb(name, shape, dt=F32):
            return ctx.enter_context(nc.sbuf_tensor(name, shape, dt))

        def sem(name):
            return ctx.enter_context(nc.semaphore(name))

        def sems(name, n=RING):
            return [sem(f"{name}{i}") for i in range(n)]

        xn = sb("xn", [P, N])
        x_head = sb("x_head", [P, N], F32R)
        x_rest = sb("x_rest", [P, N], F32R)
        x2_head = sb("x2_head", [P, N], F32R)
        x2_rest = sb("x2_rest", [P, N], F32R)
        xf = sb("xf", [P, N])
        grow = sb("grow", [P, N])
        ring = sb("ring", [P, RING, BLOCK])
        head = sb("head", [P, RING, BLOCK], F32R)
        rest = sb("rest", [P, RING, BLOCK], F32R)
        mask = sb("mask", [P, RING, BLOCK], U8)
        hT = sb("hT", [P, 2, BLOCK])
        xT = sb("xT", [P, BLOCK])
        rows = sb("rows", [P, BLOCK])
        tmp = sb("tmp", [P, BLOCK])
        stats = sb("stats", [P, SUB, 6])
        mv = sb("mv", [P, SUB, 2])
        rstd = sb("rstd", [P, SUB])
        nbias = sb("nbias", [P, SUB])
        den = sb("den", [P, SUB])
        zero = sb("zero", [P, SUB])
        rden = sb("rden", [P, SUB])
        s2 = sb("s2", [P, TILES])
        Hj = sb("Hj", [P, TILES])
        Fj = sb("Fj", [P, TILES])
        xsum = sb("xsum", [P, 2 * BLOCKS])
        small = sb("small", [P, 16])
        sc = sb("sc", [P, 24, SUB])
        wmlp_s = sb("wmlp_s", [P, 8 * D])
        bmlp_s = sb("bmlp_s", [P, 6])
        eps_s = sb("eps_s", [P, 2])
        bm_s = sb("bm_s", [P, D])
        gw_s = sb("gw_s", [P, 2 * D])
        gwt_s = sb("gwt_s", [P, 2 * D])
        glast_s = sb("glast_s", [P, 2 * D])
        ga_s = sb("ga_s", [P, 4])
        hwt_s = sb("hwt_s", [P, D + 1])
        hw_s = sb("hw_s", [P, D])
        hbias_s = sb("hbias_s", [P, D])
        hbcol_s = sb("hbcol_s", [P, 1])
        ident = sb("ident", [P, P])
        ones = sb("ones", [P, P])
        gwd = sb("gwd", [P, 2, D + 1])
        wa = sb("wa", [P, 2, 2])
        wa1 = sb("wa1", [P, 2, P])
        meanwh = sb("meanwh", [P, D])
        eyes = sb("eyes", [P, 2 * BLOCKS - 1, P], U8)
        halves = sb("halves", [P, 3 * SUB])
        eye_now = sb("eye_now", [P, BLOCKS * P], U8)
        bconst = sb("bconst", [P, 4])
        sqs = sb("sqs", [P, D])
        squares = sb("squares", [P, 3, BLOCK], mybir.dt.bfloat16)
        ps = [ctx.enter_context(nc.psum_tensor(f"ps{i}", [P, HALF], F32)) for i in range(8)]
        mask_dram = nc.dram_tensor("mask_scratch", [STREAM * P, BLOCK], U8).ap()

        consts_in = sem("consts_in")
        x_in = sem("x_in")
        x2_in = sem("x2_in")
        tile_in = [sems(f"tile_in_{k}_") for k in range(4)]
        mask_out = sems("mask_out_")
        heads = [sem(f"heads_{k}") for k in range(4)]
        rests = [sem(f"rests_{k}") for k in range(4)]
        used = [sem(f"used_{k}") for k in range(4)]
        root_asked = [sem(f"root_asked_{k}") for k in range(4)]
        root_done = [sem(f"root_done_{k}") for k in range(4)]
        bias_root = sem("bias_root")
        eye_set = sem("eye_set")
        eyed = sem("eyed")
        multiplied = [sem(f"multiplied_{k}") for k in range(4)]
        evac_a = [sem(f"evac_a_{k}") for k in range(4)]
        evac_d = [sem(f"evac_d_{k}") for k in range(4)]
        mlp_mm = sem("mlp_mm")
        natural = [sem(f"natural_{k}") for k in range(4)]
        rows_read = sem("rows_read")
        norm_ready = [sem(f"norm_ready_{k}") for k in range(4)]
        rows_done = sem("rows_done")
        final_rows = sem("final_rows")
        x_ready = [sem(f"x_ready_{k}") for k in range(4)]
        x_kept = [sem(f"x_kept_{k}") for k in range(3)]
        turned = [sem(f"turned_{k}") for k in range(4)]
        xT_ready = [sem(f"xT_ready_{k}") for k in range(4)]
        scores = [sem(f"scores_{k}") for k in range(4)]
        scored_a = [sem(f"scored_a_{k}") for k in range(4)]
        scored_d = [sem(f"scored_d_{k}") for k in range(4)]
        chain_d = [sem(f"chain_d_{k}") for k in range(6)]
        chain_a = [sem(f"chain_a_{k}") for k in range(6)]
        setup_d = sem("setup_d")
        setup_p = sem("setup_p")
        setup_a = sem("setup_a")
        setup_pe = sem("setup_pe")
        split_h = sem("split_h")
        split_r = sem("split_r")
        bm_added = sem("bm_added")
        top_d = [sem(f"top_d_{k}") for k in range(4)]
        top_pe = [sem(f"top_pe_{k}") for k in range(4)]
        top_a = [sem(f"top_a_{k}") for k in range(4)]
        g_ready = [sem(f"g_ready_{k}") for k in range(4)]
        xf_ready = [sem(f"xf_ready_{k}") for k in range(4)]
        elu_d = sem("elu_d")
        elu_a = sem("elu_a")
        hyp_d = sem("hyp_d")
        hyp_a = sem("hyp_a")
        hyp_out_a = sem("hyp_out_a")
        hyp_out_d = sem("hyp_out_d")
        fin_d = sem("fin_d")
        fin_a = sem("fin_a")
        stored = sem("stored")
        block = ctx.enter_context(nc.Block())

        def col(buf, blk, it, n=1):
            return buf[:, bass.ds(blk * BLOCK + it * P, n * P)]

        CONSTS = [(wmlp_s, wmlp), (bmlp_s, bmlp), (eps_s, eps), (bm_s, bm), (gw_s, gw), (gwt_s, gwt),
                  (glast_s, glast), (ga_s, ga), (hwt_s, hwt), (hw_s, hw), (hbias_s, hbias),
                  (hbcol_s, hbcol), (ident, ident_in)]

        @block.sync
        def _(sp):
            def tile_rows(buf, t):
                return buf[bass.ds(t * P, P), :]

            def stream(load):
                for r in range(RING):
                    load(r, r, True)
                with sp.Fori(1, STREAM // RING) as g:
                    for r in range(RING):
                        load(g * RING + r, r, False)

            sp.dma_start(xn[:, :], x).then_inc(x_in, 16)
            sp.dma_start(grow[:, :], x2).then_inc(x2_in, 16)
            for dst, src in CONSTS:
                sp.dma_start(dst[:, 0:src.shape[1]], src).then_inc(consts_in, 16)

            def load0(t, r, first):
                if not first:
                    sp.wait_ge(used[0], t - (RING - 1))
                sp.dma_start(ring[:, r, :], tile_rows(adj, t)).then_inc(tile_in[0][r], 16)
                if not first:
                    sp.dma_start(tile_rows(mask_dram, t - RING), mask[:, r, :]).then_inc(mask_out[r], 16)

            stream(load0)
            for r in range(RING):
                t = STREAM - RING + r
                sp.wait_ge(used[0], t + 1)
                sp.dma_start(tile_rows(mask_dram, t), mask[:, r, :]).then_inc(mask_out[r], 16)
            for r in range(RING):
                sp.wait_ge(mask_out[r], 16 * (STREAM // RING))

            for k in (1, 2):
                def load_mask(t, r, first):
                    if not first:
                        sp.wait_ge(used[k], t - (RING - 1))
                    elif k == 2:
                        sp.wait_ge(used[1], STREAM - RING + r + 1)
                    sp.dma_start(mask[:, r, :], tile_rows(mask_dram, t)).then_inc(tile_in[k][r], 16)

                stream(load_mask)

            def load3(t, r, first):
                if first:
                    sp.wait_ge(multiplied[2], STREAM - RING + r + 1)
                else:
                    sp.wait_ge(rests[3], t - (RING - 1))
                sp.dma_start(ring[:, r, :], tile_rows(adj, t)).then_inc(tile_in[3][r], 16)

            stream(load3)

            for blk in range(BLOCKS):
                sp.wait_ge(x_ready[3], blk + 1)
                sp.dma_start(out[:, blk * BLOCK:(blk + 1) * BLOCK], xn[:, blk * BLOCK:(blk + 1) * BLOCK]).then_inc(stored, 16)
            sp.wait_ge(stored, 16 * BLOCKS)

        @block.scalar
        def _(act):
            def split_head(k, blk, jt):
                r = jt % RING
                act.wait_ge(tile_in[k][r], (blk * (TILES // RING) + jt // RING + 1) * 16)
                if not (isinstance(blk, int) and blk == 0 and jt < RING):
                    act.wait_ge(multiplied[k], blk * TILES + jt - (RING - 1))
                nc.scalar.activation(head[:, r, :], ring[:, r, :], ACT.Copy).then_inc(heads[k], 1)

            def turn_copy(k, blk):
                for h in range(2):
                    act.wait_ge(turned[k], blk * 2 + h + 1)
                    if k == 0:
                        nc.scalar.activation(xT[:, h * HALF:(h + 1) * HALF], ps[4 + h][:, :], ACT.Copy,
                                             accum_out=xsum[:, bass.ds(blk * 2 + h, 1)]).then_inc(xT_ready[k], 1)
                    else:
                        nc.scalar.activation(xT[:, h * HALF:(h + 1) * HALF], ps[4 + h][:, :],
                                             ACT.Copy).then_inc(xT_ready[k], 1)

            def keep_s1(k, blk):
                for h in range(2):
                    act.wait_ge(scores[k], blk * 3 + h + 1)
                    nc.scalar.activation(grow[:, bass.ds(blk * BLOCK + h * HALF, HALF)], ps[6 + h][:, :],
                                         ACT.Copy).then_inc(scored_a[k], 1)

            act.wait_ge(x_in, 16)
            nc.scalar.activation(x_head[:, :], xn[:, :], ACT.Copy).then_inc(split_h, 1)
            act.wait_ge(x2_in, 16)
            nc.scalar.activation(x2_head[:, :], grow[:, :], ACT.Copy).then_inc(split_h, 1)
            act.wait_ge(bias_root, 1)
            nc.scalar.activation(bconst[:, 3:4], bconst[:, 2:3], ACT.Tanh).then_inc(setup_a, 1)

            def nothing(blk, step):
                pass

            def epilogue0(blk, step):
                if step == 3:
                    act.wait_ge(multiplied[0], (blk + 1) * TILES)
                    for h in range(2):
                        nc.scalar.activation(hT[:, 0, h * HALF:(h + 1) * HALF], ps[h][:, :], ACT.Identity,
                                             scale=small[:, 0:1]).then_inc(evac_a[0], 1)
                if 4 <= step < 10:
                    l, h = divmod(step - 4, 2)
                    act.wait_ge(mlp_mm, blk * 12 + 2 * (step - 4) + 1)
                    nc.scalar.activation(hT[:, 0, h * HALF:(h + 1) * HALF], ps[4 + h][:, :], ACT.Relu,
                                         bias=bmlp_s[:, l:l + 1]).then_inc(evac_a[0], 1)
                if step == 18:
                    turn_copy(0, blk)
                if step == 20:
                    keep_s1(0, blk)

            act.wait_ge(setup_d, 4)
            pipelined(act, lambda blk, jt: split_head(0, blk, jt), epilogue0)

            def attention_tables(k):
                act.wait_ge(top_d[k], 3)
                nc.scalar.activation(Fj[:, :], s2[:, :], ACT.Exp, bias=small[:, 6:7], scale=0.2).then_inc(top_a[k], 1)
                nc.scalar.activation(Hj[:, :], s2[:, :], ACT.Exp, bias=small[:, 5:6], scale=0.8).then_inc(top_a[k], 1)
                for b in range(BLOCKS):
                    act.wait_ge(top_d[k], 4 + b)
                    nc.scalar.activation(grow[:, b * BLOCK:(b + 1) * BLOCK], grow[:, b * BLOCK:(b + 1) * BLOCK],
                                         ACT.Exp, scale=-0.8).then_inc(g_ready[k], 1)

            attention_tables(1)

            def epilogue1(blk, step):
                if step == 3:
                    act.wait_ge(multiplied[1], (blk + 1) * TILES)
                    nc.scalar.activation(hT[:, 0, 0:HALF], ps[0][:, :], ACT.Copy).then_inc(evac_a[1], 1)
                if step == 7:
                    act.wait_ge(elu_d, blk + 1)
                    nc.scalar.activation(tmp[:, :], tmp[:, :], ACT.Exp).then_inc(elu_a, 1)
                if step == 15:
                    turn_copy(1, blk)
                if step == 17:
                    keep_s1(1, blk)

            pipelined(act, nothing, epilogue1)

            def square_sums(src, place, junk):
                for it in range(SUB):
                    last = nc.scalar.activation(squares[:, junk, it * P:(it + 1) * P], src[:, it * P:(it + 1) * P], ACT.Square,
                                                accum_out=sc[:, place, it:it + 1])
                return last

            def apply_norm(k, blk, dst):
                act.wait_ge(norm_ready[k], blk + 1)
                for it in range(SUB):
                    last = nc.scalar.activation(dst(it), rows[:, it * P:(it + 1) * P], ACT.Identity,
                                                bias=nbias[:, it:it + 1], scale=rstd[:, it:it + 1])
                last.then_inc(x_ready[k], 1)

            attention_tables(2)

            def epilogue2(blk, step):
                if step == 3:
                    act.wait_ge(multiplied[2], (blk + 1) * TILES)
                    for h in range(2):
                        nc.scalar.activation(hT[:, 0, h * HALF:(h + 1) * HALF], ps[h][:, :], ACT.Copy).then_inc(evac_a[2], 1)
                if step == 8:
                    apply_norm(2, blk, lambda it: rows[:, it * P:(it + 1) * P])
                if step == 9:
                    act.wait_ge(x_ready[2], blk + 1)
                    nc.scalar.activation(col(xn, blk, 0, SUB), rows[:, :], ACT.Copy).then_inc(x_kept[2], 1)
                if step == 10:
                    turn_copy(2, blk)
                if step == 11:
                    square_sums(rows, 0, 0).then_inc(hyp_a, 1)
                if step == 12:
                    for b in range(3):
                        n = min(3, SUB - 3 * b)
                        act.wait_ge(scores[2], blk * 3 + b + 1)
                        src = ps[4 + b][:, 0:390].rearrange("p (t c) -> p t c", c=130)
                        nc.scalar.activation(sc[:, 2, 3 * b:3 * b + n], src[:, 0:n, D], ACT.Copy)
                        nc.scalar.activation(tmp[:, 3 * b * P:(3 * b + n) * P].rearrange("p (t c) -> p t c", c=P),
                                             src[:, 0:n, 0:D], ACT.Copy).then_inc(scored_a[2], 1)
                if step == 13:
                    act.wait_ge(scored_a[2], blk * 3 + 3)
                    square_sums(tmp, 1, 1).then_inc(hyp_a, 1)
                if step == 15:
                    act.wait_ge(hyp_d, blk * 6 + 1)
                    nc.scalar.activation(sc[:, 9, :], sc[:, 8, :], ACT.Ln).then_inc(hyp_a, 1)
                if step == 17:
                    act.wait_ge(hyp_d, blk * 6 + 2)
                    nc.scalar.activation(sc[:, 6, :], sc[:, 5, :], ACT.Tanh).then_inc(hyp_a, 1)
                if step == 19:
                    act.wait_ge(hyp_d, blk * 6 + 3)
                    for it in range(SUB):
                        last = nc.scalar.activation(rows[:, it * P:(it + 1) * P], hbias_s[:, :], ACT.Copy, scale=sc[:, 17, it:it + 1])
                    last.then_inc(hyp_a, 1)
                if step == 21:
                    act.wait_ge(hyp_d, blk * 6 + 4)
                    square_sums(tmp, 0, 2).then_inc(hyp_a, 1)
                if step == 23:
                    act.wait_ge(hyp_d, blk * 6 + 5)
                    nc.scalar.activation(sc[:, 9, :], sc[:, 8, :], ACT.Ln).then_inc(hyp_a, 1)
                if step == 25:
                    act.wait_ge(hyp_d, blk * 6 + 6)
                    for it in range(SUB):
                        last = nc.scalar.activation(col(x_head, blk, it), tmp[:, it * P:(it + 1) * P], ACT.Copy,
                                                    scale=sc[:, 16, it:it + 1])
                    last.then_inc(hyp_out_a, 1)

            pipelined(act, nothing, epilogue2)

            def epilogue3(blk, step):
                if step == 3:
                    act.wait_ge(multiplied[3], (blk + 1) * TILES)
                    for h in range(2):
                        nc.scalar.activation(hT[:, 0, h * HALF:(h + 1) * HALF], ps[h][:, :], ACT.Copy).then_inc(evac_a[3], 1)
                if step == 4:
                    for h in range(2):
                        act.wait_ge(natural[3], blk * 2 + h + 1)
                        nc.scalar.activation(rows[:, h * HALF:(h + 1) * HALF], ps[4 + h][:, :], ACT.Copy).then_inc(rows_read, 1)
                        nc.scalar.activation(tmp[:, h * HALF:(h + 1) * HALF], ps[4 + h][:, :], ACT.Relu).then_inc(rows_read, 1)
                if step == 5:
                    act.wait_ge(rows_read, blk * 4 + 4)
                    square_sums(rows, 0, 0).then_inc(fin_a, 1)
                if step == 6:
                    square_sums(tmp, 1, 1).then_inc(fin_a, 1)
                if step == 8:
                    act.wait_ge(fin_d, blk + 1)
                    nc.scalar.activation(sc[:, 5, :], sc[:, 4, :], ACT.Tanh).then_inc(fin_a, 1)
                if step == 12:
                    apply_norm(3, blk, lambda it: col(xn, blk, it))

            pipelined(act, lambda blk, jt: split_head(3, blk, jt), epilogue3)

        @block.gpsimd
        def _(pool):
            nc.gpsimd.memset(ones[:, :], 1.0).then_inc(setup_p, 1)
            nc.gpsimd.memset(eyes[:, :, :], 0).then_inc(setup_p, 1)
            nc.gpsimd.memset(small[:, :], 0.0).then_inc(setup_p, 1)
            nc.gpsimd.memset(halves[:, 0:2 * SUB], 0.5).then_inc(setup_p, 1)
            nc.gpsimd.memset(halves[:, 2 * SUB:], -0.5).then_inc(setup_p, 1)
            nc.gpsimd.memset(gwd[:, :, :], 0.0).then_inc(setup_p, 1)
            pool.wait_ge(setup_p, 6)
            pool.wait_ge(consts_in, 16 * len(CONSTS))
            nc.gpsimd.tensor_copy(eyes[:, BLOCKS - 1, :], ident[:, :]).then_inc(setup_p, 1)
            pool.wait_ge(setup_p, 6)
            pool.wait_ge(setup_d, 3)
            nc.gpsimd.tensor_tensor(bconst[:, 2:3], bconst[:, 2:3], halves[:, 0:1], ALU.pow).then_inc(bias_root, 1)
            pool.wait_ge(split_r, 1)
            nc.gpsimd.tensor_tensor(xn[:, :].rearrange("p (t d) -> p t d", d=D), xn[:, :].rearrange("p (t d) -> p t d", d=D),
                                    bm_s[:, :].unsqueeze(1).broadcast_to([P, TILES, D]), ALU.add).then_inc(bm_added, 1)

            def root(k, blk, n, buf, exponent):
                pool.wait_ge(root_asked[k], blk * ROOTS[k] + n)
                nc.gpsimd.tensor_tensor(buf, buf, exponent, ALU.pow).then_inc(root_done[k], 1)

            half, minus_half = halves[:, 0:SUB], halves[:, 2 * SUB:3 * SUB]
            two_halves = halves[:, 0:2 * SUB].rearrange("p (a b) -> p a b", a=2)
            for k in range(2):
                with pool.Fori(0, BLOCKS) as blk:
                    root(k, blk, 1, rstd[:, :], minus_half)

            with pool.Fori(0, BLOCKS) as blk:
                root(2, blk, 1, rstd[:, :], minus_half)
                root(2, blk, 2, sc[:, 3:5, :], two_halves)
                root(2, blk, 3, sc[:, 3, :], half)

            with pool.Fori(0, BLOCKS) as blk:
                root(3, blk, 1, sc[:, 0:2, :], two_halves)
                root(3, blk, 2, rstd[:, :], minus_half)
        @block.vector
        def _(dve):
            def rest_of(k, blk, jt):
                r = jt % RING
                first = isinstance(blk, int) and jt < RING
                dve.wait_ge(heads[k], blk * TILES + jt + 1)
                if not first:
                    dve.wait_ge(multiplied[k], blk * TILES + jt - (RING - 1))
                nc.vector.tensor_tensor(rest[:, r, :], ring[:, r, :], head[:, r, :].bitcast(F32),
                                        ALU.subtract).then_inc(rests[k], 1)
                if k == 0:
                    if not first:
                        dve.wait_ge(mask_out[r], (blk * (TILES // RING) + jt // RING) * 16)
                    nc.vector.tensor_scalar(mask[:, r, :], ring[:, r, :], 0.0, None, ALU.is_gt).then_inc(used[k], 1)

            def weigh(k, blk, jt):
                r = jt % RING
                dve.wait_ge(tile_in[k][r], (blk * (TILES // RING) + jt // RING + 1) * 16)
                if k == 2:
                    c = jt // SUB
                    part = mask[:, r, (jt % SUB) * P:(jt % SUB + 1) * P]
                    nc.vector.tensor_tensor(part, part, eye_now[:, c * P:(c + 1) * P], ALU.max).then_inc(eyed, 1)
                    dve.wait_ge(eyed, blk * TILES + jt + 1)
                if not (isinstance(blk, int) and jt < RING):
                    dve.wait_ge(multiplied[k], blk * TILES + jt - (RING - 1))
                nc.vector.scalar_tensor_tensor(ring[:, r, :], grow[:, bass.ds(blk * BLOCK, BLOCK)], Hj[:, jt:jt + 1],
                                               mask[:, r, :], ALU.max, ALU.mult).then_inc(used[k], 1)

            def row_stats(ch, its=range(SUB)):
                for it in its:
                    last = nc.vector.bn_stats(stats[:, it, :], rows[:, it * P:(it + 1) * P])
                ch.step(last)

            def deviation(k, ch):
                nc.vector.memset(small[:, 14:15], 0.0)
                for it in range(SUB):
                    last = nc.vector.bn_aggr(mv[:, it, :], stats[:, it, :])
                ch.step(last)
                nc.vector.tensor_scalar(rstd[:, :], mv[:, :, 1], LN_EPS, None, ALU.add).then_inc(root_asked[k], 1)

            def norm_bias(k, blk):
                dve.wait_ge(root_done[k], blk * ROOTS[k] + (2 if k == 3 else 1))
                nc.vector.scalar_tensor_tensor(nbias[:, :], mv[:, :, 0], -1.0, rstd[:, :], ALU.mult, ALU.mult).then_inc(norm_ready[k], 1)

            def normalise(k, blk):
                dve.wait_ge(root_done[k], blk + 1)
                for it in range(SUB):
                    r = rows[:, it * P:(it + 1) * P]
                    last = nc.vector.tensor_scalar(r, r, mv[:, it, 0:1], rstd[:, it:it + 1], ALU.subtract, ALU.mult)
                last.then_inc(x_ready[k], 1)

            def keep_rows(k, blk):
                dve.wait_ge(x_ready[k], blk + 1)
                nc.vector.tensor_scalar(col(xn, blk, 0, SUB), rows[:, :], 1.0, None, ALU.mult).then_inc(x_kept[k], 1)

            def keep_s2(k, blk):
                dve.wait_ge(scores[k], blk * 3 + 3)
                nc.vector.tensor_copy(s2[:, bass.ds(blk * SUB, SUB)], ps[4][:, 0:SUB]).then_inc(scored_d[k], 1)

            dve.wait_ge(split_h, 1)
            nc.vector.tensor_tensor(x_rest[:, :], xn[:, :], x_head[:, :].bitcast(F32), ALU.subtract).then_inc(split_r, 1)
            dve.wait_ge(split_h, 2)
            nc.vector.tensor_tensor(x2_rest[:, :], grow[:, :], x2_head[:, :].bitcast(F32), ALU.subtract).then_inc(split_r, 1)
            dve.wait_ge(setup_p, 7)
            dve.wait_ge(consts_in, 16 * len(CONSTS))
            nc.vector.tensor_tensor(sqs[:, :], hbias_s[:, :], hbias_s[:, :], ALU.mult).then_inc(setup_d, 1)
            dve.wait_ge(setup_d, 1)
            nc.vector.reduce_sum(bconst[:, 0:1], sqs[:, :], AX.X).then_inc(setup_d, 1)
            dve.wait_ge(setup_d, 2)
            nc.vector.tensor_scalar(bconst[:, 2:3], bconst[:, 0:1], MIN_NORM ** 2, None, ALU.max).then_inc(setup_d, 1)
            nc.vector.tensor_scalar(small[:, 0:2], eps_s[:, :], 2.0, None, ALU.add).then_inc(setup_d, 1)
            dve.wait_ge(setup_d, 4)
            dve.wait_ge(setup_a, 1)
            nc.vector.reciprocal(bconst[:, 2:3], bconst[:, 2:3]).then_inc(setup_d, 1)
            dve.wait_ge(setup_d, 5)
            nc.vector.scalar_tensor_tensor(bconst[:, 1:2], bconst[:, 3:4], MAX_NORM, bconst[:, 2:3], ALU.min, ALU.mult).then_inc(setup_d, 1)
            dve.wait_ge(setup_d, 6)
            nc.vector.scalar_tensor_tensor(bconst[:, 2:3], bconst[:, 1:2], bconst[:, 0:1], bconst[:, 1:2], ALU.mult, ALU.mult).then_inc(setup_d, 1)
            for l in range(2):
                nc.vector.tensor_tensor(gwd[:, l, 0:D], gw_s[:, l * D:(l + 1) * D], glast_s[:, l * D:(l + 1) * D], ALU.subtract).then_inc(setup_d, 1)
                nc.vector.tensor_copy(gwd[:, l, D:D + 1], ident[:, P - 1:P]).then_inc(setup_d, 1)
            dve.wait_ge(setup_pe, 1)
            nc.vector.tensor_copy(wa[:, :, :].rearrange("p a b -> p (a b)"), ps[7][:, 0:4]).then_inc(setup_d, 1)
            nc.vector.tensor_copy(hwt_s[:, D:D + 1], ps[7][:, 4:5]).then_inc(setup_d, 1)
            dve.wait_ge(setup_d, 13)
            for l in range(2):
                nc.vector.tensor_scalar(wa1[:, l, :], ones[:, :], wa[:, l, 0:1], None, ALU.mult).then_inc(setup_d, 1)
            SETUP_D = 15
            dve.wait_ge(setup_d, SETUP_D)

            ch0 = Chain(dve, chain_d[0], 9)

            def epilogue0(blk, step):
                if step == 3:
                    dve.wait_ge(multiplied[0], (blk + 1) * TILES)
                    for h in range(2):
                        nc.vector.tensor_scalar(hT[:, 1, h * HALF:(h + 1) * HALF], ps[2 + h][:, :], small[:, 1:2], None,
                                                ALU.mult).then_inc(evac_d[0], 1)
                if 4 <= step < 10:
                    l, h = divmod(step - 4, 2)
                    dve.wait_ge(mlp_mm, blk * 12 + 2 * (step - 4) + 2)
                    nc.vector.tensor_scalar(hT[:, 1, h * HALF:(h + 1) * HALF], ps[6 + h][:, :], bmlp_s[:, 3 + l:4 + l],
                                            0.0, ALU.add, ALU.max).then_inc(evac_d[0], 1)
                if 11 <= step < 15:
                    b = step - 11
                    dve.wait_ge(natural[0], blk * 4 + b + 1)
                    ch0.step(nc.vector.tensor_tensor(rows[:, b * 256:(b + 1) * 256], ps[4 + b][:, 0:256], col(xn, blk, 2 * b, 2), ALU.add))
                    row_stats(ch0, (2 * b, 2 * b + 1))
                if step == 15:
                    deviation(0, ch0)
                if step == 16:
                    normalise(0, blk)
                if step == 17:
                    keep_rows(0, blk)
                if step == 20:
                    keep_s2(0, blk)

            dve.wait_ge(bm_added, 1)
            pipelined(dve, lambda blk, jt: rest_of(0, blk, jt), epilogue0, ch0)

            def attention_top(k):
                dve.wait_ge(scored_d[k - 1], BLOCKS)
                dve.wait_ge(x_kept[k - 1], BLOCKS)
                nc.vector.reduce_max(small[:, 2:3], s2[:, :], AX.X).then_inc(top_d[k], 1)
                dve.wait_ge(top_pe[k], 1)
                nc.vector.reduce_max(small[0:1, 3:4], ps[4][0:1, 0:P], AX.X).then_inc(top_d[k], 1)
                dve.wait_ge(top_pe[k], 2)
                ch = Chain(dve, chain_d[3 + k])
                nc.vector.tensor_copy(small[:, 4:5], ps[5][:, 0:1])
                nc.vector.tensor_scalar(small[:, 6:7], ps[5][:, 0:1], -0.2, None, ALU.mult)
                ch.step(nc.vector.tensor_scalar(small[:, 5:6], ps[5][:, 0:1], -0.8, None, ALU.mult))
                nc.vector.memset(small[:, 14:15], 0.0).then_inc(top_d[k], 1)
                dve.wait_ge(scored_a[k - 1], 2 * BLOCKS)
                for b in range(BLOCKS):
                    nc.vector.tensor_scalar(grow[:, b * BLOCK:(b + 1) * BLOCK], grow[:, b * BLOCK:(b + 1) * BLOCK],
                                            small[:, 4:5], 0.0, ALU.add, ALU.max).then_inc(top_d[k], 1)
                dve.wait_ge(top_a[k], 1)
                for b in range(BLOCKS):
                    xv = xn[:, b * BLOCK:(b + 1) * BLOCK].rearrange("p (t d) -> p t d", d=D)
                    xo = xf[:, b * BLOCK:(b + 1) * BLOCK].rearrange("p (t d) -> p t d", d=D)
                    fv = Fj[:, b * SUB:(b + 1) * SUB].unsqueeze(2)
                    nc.vector.tensor_tensor(xo[:, :, 0:D - 1], xv[:, :, 0:D - 1], fv.broadcast_to([P, SUB, D - 1]), ALU.mult)
                    nc.vector.tensor_copy(xo[:, :, D - 1:D], fv).then_inc(xf_ready[k], 1)
                if k == 1:
                    ch.step(nc.vector.reduce_sum(small[:, 7:8], xsum[:, :], AX.X))
                    nc.vector.tensor_scalar(sqs[:, :], ones[:, :], small[:, 7:8], 1.0 / N, ALU.mult, ALU.mult).then_inc(top_d[k], 1)
                    dve.wait_ge(top_pe[k], 3)
                    nc.vector.tensor_copy(meanwh[:, :], ps[6][:, 0:D]).then_inc(top_d[k], 1)
                dve.wait_ge(top_a[k], 2)

            def denominators(k, blk, ch):
                for b in range(3):
                    n = min(3, SUB - 3 * b)
                    dve.wait_ge(natural[k], blk * 3 + b + 1)
                    src = ps[4 + b][:, 0:390].rearrange("p (t c) -> p t c", c=130)[:, 0:n, D]
                    last = nc.vector.tensor_copy(den[:, 3 * b:3 * b + n], src)
                ch.step(last)
                ch.step(nc.vector.tensor_scalar(zero[:, :], den[:, :], 0.0, None, ALU.is_equal))
                ch.step(nc.vector.tensor_tensor(den[:, :], den[:, :], zero[:, :], ALU.add))
                ch.step(nc.vector.reciprocal(rden[:, :], den[:, :]))

            def nat(it):
                return ps[4 + it // 3][:, (it % 3) * 130:(it % 3) * 130 + D]

            attention_top(1)
            ch1 = Chain(dve, chain_d[1], 10)

            def stream1(blk, jt):
                if isinstance(blk, int) and jt == 0:
                    dve.wait_ge(g_ready[1], BLOCKS)
                weigh(1, blk, jt)

            def epilogue1(blk, step):
                if step == 3:
                    dve.wait_ge(multiplied[1], (blk + 1) * TILES)
                    nc.vector.tensor_copy(hT[:, 0, HALF:], ps[1][:, :]).then_inc(evac_d[1], 1)
                if step == 4:
                    denominators(1, blk, ch1)
                if step == 5:
                    for it in range(SUB):
                        last = nc.vector.tensor_scalar(rows[:, it * P:(it + 1) * P], nat(it), rden[:, it:it + 1], None, ALU.mult)
                    ch1.step(last)
                if step == 6:
                    for it in range(SUB):
                        last = nc.vector.scalar_tensor_tensor(rows[:, it * P:(it + 1) * P], meanwh[:, :], zero[:, it:it + 1],
                                                              rows[:, it * P:(it + 1) * P], ALU.mult, ALU.add)
                    ch1.step(last)
                if step == 7:
                    nc.vector.tensor_scalar(tmp[:, :], rows[:, :], 0.0, None, ALU.min).then_inc(elu_d, 1)
                    ch1.step(nc.vector.scalar_tensor_tensor(rows[:, :], rows[:, :], 0.0, col(xn, blk, 0, SUB), ALU.max, ALU.add))
                if step == 9:
                    dve.wait_ge(elu_a, blk + 1)
                    ch1.step(nc.vector.scalar_tensor_tensor(rows[:, :], tmp[:, :], -1.0, rows[:, :], ALU.add, ALU.add))
                if step == 10:
                    row_stats(ch1)
                if step == 11:
                    deviation(1, ch1)
                if step == 13:
                    normalise(1, blk)
                if step == 14:
                    keep_rows(1, blk)
                if step == 17:
                    keep_s2(1, blk)

            pipelined(dve, stream1, epilogue1, ch1)

            attention_top(2)
            ch2 = Chain(dve, chain_d[2], 36)

            def artanh_ln(ch, t):
                ch.step(nc.vector.tensor_scalar(sc[:, 10, :], sc[:, t, :], -1.0, 1.0, ALU.mult, ALU.add))
                ch.step(nc.vector.reciprocal(sc[:, 10, :], sc[:, 10, :]))
                ch.step(nc.vector.scalar_tensor_tensor(sc[:, 7, :], sc[:, t, :], 2.0, sc[:, 10, :], ALU.mult, ALU.mult))
                nc.vector.tensor_scalar(sc[:, 8, :], sc[:, 7, :], 1.0, None, ALU.add).then_inc(hyp_d, 1)

            def artanh_rest(ch, o, asked, ln):
                dve.wait_ge(hyp_d, asked)
                ch.step(nc.vector.tensor_scalar(sc[:, 10, :], sc[:, 8, :], -1.0, None, ALU.add))
                ch.step(nc.vector.tensor_scalar(sc[:, 11, :], sc[:, 10, :], 0.0, None, ALU.is_equal))
                ch.step(nc.vector.tensor_tensor(sc[:, 10, :], sc[:, 10, :], sc[:, 11, :], ALU.add))
                ch.step(nc.vector.reciprocal(sc[:, 10, :], sc[:, 10, :]))
                dve.wait_ge(hyp_a, ln)
                ch.step(nc.vector.tensor_tensor(sc[:, 9, :], sc[:, 9, :], sc[:, 11, :], ALU.add))
                ch.step(nc.vector.tensor_tensor(sc[:, 9, :], sc[:, 9, :], sc[:, 10, :], ALU.mult))
                ch.step(nc.vector.scalar_tensor_tensor(sc[:, o, :], sc[:, 7, :], 0.5, sc[:, 9, :], ALU.mult, ALU.mult))

            def stream2(blk, jt):
                if jt == 0:
                    if isinstance(blk, int):
                        dve.wait_ge(g_ready[2], BLOCKS)
                    nc.vector.tensor_scalar(eye_now[:, :], eyes[:, :, :].rearrange("p a b -> p (a b)")[
                        :, bass.ds(blk * -P + (BLOCKS - 1) * P, BLOCKS * P)], 0.0, None, ALU.max).then_inc(eye_set, 1)
                    dve.wait_ge(eye_set, blk + 1)
                weigh(2, blk, jt)

            def epilogue2(blk, step):
                if step == 4:
                    denominators(2, blk, ch2)
                if step == 5:
                    for it in range(SUB):
                        last = nc.vector.scalar_tensor_tensor(rows[:, it * P:(it + 1) * P], nat(it), rden[:, it:it + 1],
                                                              col(xn, blk, it), ALU.mult, ALU.add)
                    last.then_inc(rows_done, 1)
                    dve.wait_ge(rows_done, blk + 1)
                if step == 6:
                    row_stats(ch2)
                if step == 7:
                    deviation(2, ch2)
                if step == 8:
                    norm_bias(2, blk)
                if step == 14:
                    dve.wait_ge(hyp_a, blk * 7 + 2)
                    nc.vector.tensor_scalar(sc[:, 3:5, :], sc[:, 0:2, :], MIN_NORM ** 2, None, ALU.max).then_inc(root_asked[2], 1)
                if step == 15:
                    dve.wait_ge(root_done[2], blk * 3 + 2)
                    nc.vector.reciprocal(sc[:, 12, :], sc[:, 3, :])
                    nc.vector.reciprocal(sc[:, 13, :], sc[:, 4, :])
                    ch2.step(nc.vector.tensor_scalar(sc[:, 14, :], sc[:, 3, :], CLIP, None, ALU.min))
                    artanh_ln(ch2, 14)
                if step == 17:
                    artanh_rest(ch2, 15, blk * 6 + 1, blk * 7 + 3)
                    ch2.step(nc.vector.tensor_tensor(sc[:, 12, :], sc[:, 4, :], sc[:, 12, :], ALU.mult))
                    nc.vector.tensor_tensor(sc[:, 5, :], sc[:, 12, :], sc[:, 15, :], ALU.mult).then_inc(hyp_d, 1)
                if step == 19:
                    dve.wait_ge(hyp_a, blk * 7 + 4)
                    ch2.step(nc.vector.scalar_tensor_tensor(sc[:, 6, :], sc[:, 6, :], MAX_NORM, sc[:, 13, :], ALU.min, ALU.mult))
                    ch2.step(nc.vector.tensor_tensor(sc[:, 12, :], sc[:, 6, :], sc[:, 6, :], ALU.mult))
                    nc.vector.tensor_tensor(sc[:, 12, :], sc[:, 12, :], sc[:, 1, :], ALU.mult)
                    ch2.step(nc.vector.scalar_tensor_tensor(sc[:, 13, :], sc[:, 2, :], bconst[:, 1:2], sc[:, 6, :], ALU.mult, ALU.mult))
                    ch2.step(nc.vector.tensor_scalar(sc[:, 14, :], sc[:, 13, :], 2.0, 1.0, ALU.mult, ALU.add))
                    nc.vector.scalar_tensor_tensor(sc[:, 15, :], sc[:, 14, :], bconst[:, 2:3], sc[:, 6, :], ALU.add, ALU.mult)
                    nc.vector.tensor_scalar(sc[:, 17, :], sc[:, 12, :], -1.0, 1.0, ALU.mult, ALU.add)
                    ch2.step(nc.vector.scalar_tensor_tensor(sc[:, 18, :], sc[:, 12, :], bconst[:, 2:3], sc[:, 14, :], ALU.mult, ALU.add))
                    ch2.step(nc.vector.tensor_scalar(sc[:, 18, :], sc[:, 18, :], MIN_NORM, None, ALU.max))
                    ch2.step(nc.vector.reciprocal(sc[:, 18, :], sc[:, 18, :]))
                    nc.vector.tensor_tensor(sc[:, 15, :], sc[:, 15, :], sc[:, 18, :], ALU.mult)
                    nc.vector.scalar_tensor_tensor(sc[:, 17, :], sc[:, 17, :], bconst[:, 1:2], sc[:, 18, :], ALU.mult, ALU.mult).then_inc(hyp_d, 1)
                if step == 21:
                    dve.wait_ge(hyp_d, blk * 6 + 3)
                    dve.wait_ge(hyp_a, blk * 7 + 5)
                    for it in range(SUB):
                        t = tmp[:, it * P:(it + 1) * P]
                        last = nc.vector.scalar_tensor_tensor(t, t, sc[:, 15, it:it + 1], rows[:, it * P:(it + 1) * P], ALU.mult, ALU.add)
                    last.then_inc(hyp_d, 1)
                if step == 22:
                    dve.wait_ge(hyp_a, blk * 7 + 6)
                    nc.vector.tensor_scalar(sc[:, 3, :], sc[:, 0, :], MIN_NORM ** 2, None, ALU.max).then_inc(root_asked[2], 1)
                if step == 23:
                    dve.wait_ge(root_done[2], blk * 3 + 3)
                    nc.vector.reciprocal(sc[:, 12, :], sc[:, 3, :])
                    ch2.step(nc.vector.tensor_scalar(sc[:, 14, :], sc[:, 3, :], MAX_NORM, None, ALU.min))
                    artanh_ln(ch2, 14)
                if step == 25:
                    artanh_rest(ch2, 15, blk * 6 + 5, blk * 7 + 7)
                    nc.vector.tensor_tensor(sc[:, 16, :], sc[:, 15, :], sc[:, 12, :], ALU.mult).then_inc(hyp_d, 1)
                if step == 27:
                    dve.wait_ge(hyp_d, blk * 6 + 6)
                    dve.wait_ge(hyp_out_a, blk + 1)
                    for it in range(SUB):
                        last = nc.vector.scalar_tensor_tensor(col(x_rest, blk, it), tmp[:, it * P:(it + 1) * P], sc[:, 16, it:it + 1],
                                                              col(x_head, blk, it).bitcast(F32), ALU.mult, ALU.subtract)
                    last.then_inc(hyp_out_d, 1)

            pipelined(dve, stream2, epilogue2, ch2)

            ch3 = Chain(dve, chain_d[3], 8)

            def epilogue3(blk, step):
                if step == 7:
                    dve.wait_ge(fin_a, blk * 3 + 2)
                    nc.vector.tensor_scalar(sc[:, 0:2, :], sc[:, 0:2, :], MIN_NORM ** 2, None, ALU.max).then_inc(root_asked[3], 1)
                if step == 8:
                    dve.wait_ge(root_done[3], blk * 2 + 1)
                    ch3.step(nc.vector.reciprocal(sc[:, 3, :], sc[:, 0, :]))
                    ch3.step(nc.vector.scalar_tensor_tensor(sc[:, 2, :], sc[:, 0, :], ATANH_MAX, sc[:, 3, :], ALU.min, ALU.mult))
                    ch3.step(nc.vector.tensor_tensor(sc[:, 4, :], sc[:, 1, :], sc[:, 2, :], ALU.mult))
                    nc.vector.tensor_scalar(sc[:, 4, :], sc[:, 4, :], MIN_NORM, None, ALU.max).then_inc(fin_d, 1)
                if step == 9:
                    dve.wait_ge(fin_d, blk + 1)
                    ch3.step(nc.vector.reciprocal(sc[:, 6, :], sc[:, 4, :]))
                    dve.wait_ge(fin_a, blk * 3 + 3)
                    ch3.step(nc.vector.scalar_tensor_tensor(sc[:, 5, :], sc[:, 5, :], MAX_NORM, sc[:, 6, :], ALU.min, ALU.mult))
                    ch3.step(nc.vector.tensor_tensor(sc[:, 5, :], sc[:, 5, :], sc[:, 2, :], ALU.mult))
                    for it in range(SUB):
                        last = nc.vector.scalar_tensor_tensor(rows[:, it * P:(it + 1) * P], tmp[:, it * P:(it + 1) * P], sc[:, 5, it:it + 1],
                                                              col(xn, blk, it), ALU.mult, ALU.add)
                    last.then_inc(final_rows, 1)
                    dve.wait_ge(final_rows, blk + 1)
                if step == 10:
                    row_stats(ch3)
                if step == 11:
                    deviation(3, ch3)
                if step == 12:
                    norm_bias(3, blk)

            pipelined(dve, lambda blk, jt: rest_of(3, blk, jt), epilogue3, ch3)

        @block.tensor
        def _(pe):
            pe.wait_ge(consts_in, 16 * len(CONSTS))
            for l in range(2):
                nc.tensor.matmul(ps[7][:, 2 * l:2 * l + 2], gwt_s[:, l * D:(l + 1) * D], ga_s[:, 2 * l:2 * l + 2], start=True, stop=True)
            nc.tensor.matmul(ps[7][:, 4:5], hw_s[:, :], hbcol_s[:, :], start=True, stop=True).then_inc(setup_pe, 1)
            pe.wait_ge(split_h, 2)
            pe.wait_ge(split_r, 2)
            pe.wait_ge(setup_d, 15)

            def split_products(k, blk, jt, operands):
                r = jt % RING
                j = slice(jt * P, (jt + 1) * P)
                pe.wait_ge(heads[k], blk * TILES + jt + 1)
                for n, (xh, xr) in enumerate(operands):
                    for w, st in ((xh, jt == 0), (xr, False)):
                        for h in range(2):
                            nc.tensor.matmul(ps[2 * n + h][:, :], w[:, j], head[:, r, h * HALF:(h + 1) * HALF],
                                             start=st, stop=False)
                pe.wait_ge(rests[k], blk * TILES + jt + 1)
                for n, (xh, xr) in enumerate(operands):
                    for h in range(2):
                        last = nc.tensor.matmul(ps[2 * n + h][:, :], xh[:, j], rest[:, r, h * HALF:(h + 1) * HALF],
                                                start=False, stop=(jt == TILES - 1))
                last.then_inc(multiplied[k], 1)

            def turn(k, blk):
                pe.wait_ge(x_ready[k], blk + 1)
                for h in range(2):
                    for q in range(4):
                        last = nc.tensor.transpose(ps[4 + h][:, q * P:(q + 1) * P], rows[:, (4 * h + q) * P:(4 * h + q + 1) * P], ident[:, :])
                    last.then_inc(turned[k], 1)

            def score(k, blk):
                l = k
                for h in range(2):
                    pe.wait_ge(xT_ready[k], blk * 2 + h + 1)
                    nc.tensor.matmul(ps[6 + h][:, :], wa1[:, l, :], xT[:, h * HALF:(h + 1) * HALF],
                                     start=True, stop=True).then_inc(scores[k], 1)
                for it in range(SUB):
                    last = nc.tensor.matmul(ps[4][:, it:it + 1], xT[:, it * P:(it + 1) * P], wa[:, l, 1:2], start=True, stop=True)
                last.then_inc(scores[k], 1)

            def stream0(blk, jt):
                if jt == 0 and not isinstance(blk, int):
                    pe.wait_ge(evac_a[0], blk * 8 - 6)
                    pe.wait_ge(evac_d[0], blk * 8 - 6)
                split_products(0, blk, jt, ((x_head, x_rest), (x2_head, x2_rest)))

            def epilogue0(blk, step):
                if 1 <= step < 7:
                    l, h = divmod(step - 1, 2)
                    for n, evac in ((0, evac_a), (1, evac_d)):
                        pe.wait_ge(evac[0], blk * 8 + 2 * l + h + 1)
                        w = (3 * n + l) * D
                        nc.tensor.matmul(ps[4 + 2 * n + h][:, :], wmlp_s[:, w:w + D], hT[:, n, h * HALF:(h + 1) * HALF],
                                         start=True, stop=True).then_inc(mlp_mm, 1)
                if 8 <= step < 12:
                    b = step - 8
                    pe.wait_ge(evac_a[0], blk * 8 + 8)
                    pe.wait_ge(evac_d[0], blk * 8 + 8)
                    for it in (2 * b, 2 * b + 1):
                        for n in range(2):
                            last = nc.tensor.matmul(ps[4 + b][:, (it % 2) * P:(it % 2 + 1) * P], hT[:, n, it * P:(it + 1) * P],
                                                    wmlp_s[:, (6 + n) * D:(7 + n) * D], start=(n == 0), stop=(n == 1))
                    last.then_inc(natural[0], 1)
                if step == 15:
                    turn(0, blk)
                if step == 17:
                    score(0, blk)

            pipelined(pe, stream0, epilogue0)

            def attention_top(k):
                pe.wait_ge(top_d[k], 1)
                pe.wait_ge(scored_a[k - 1], 2 * BLOCKS)
                nc.tensor.transpose(ps[4][0:1, 0:P], small[:, 2:3], ident[:, :]).then_inc(top_pe[k], 1)
                pe.wait_ge(top_d[k], 2)
                nc.tensor.matmul(ps[5][:, 0:1], ones[0:1, :], small[0:1, 3:4], start=True, stop=True).then_inc(top_pe[k], 1)
                if k == 1:
                    pe.wait_ge(top_d[k], 8)
                    nc.tensor.matmul(ps[6][:, 0:D], sqs[:, :], gw_s[:, 0:D], start=True, stop=True).then_inc(top_pe[k], 1)
                    pe.wait_ge(top_d[k], 9)

            def attention_stream(k, blk, jt):
                if jt == 0 and not isinstance(blk, int):
                    pe.wait_ge(evac_a[k], blk * (k))
                    if k == 1:
                        pe.wait_ge(evac_d[k], blk)
                if isinstance(blk, int) and jt % SUB == 0:
                    pe.wait_ge(xf_ready[k], jt // SUB + 1)
                pe.wait_ge(used[k], blk * TILES + jt + 1)
                for h in range(2):
                    last = nc.tensor.matmul(ps[h][:, :], xf[:, jt * P:(jt + 1) * P], ring[:, jt % RING, h * HALF:(h + 1) * HALF],
                                            start=(jt == 0), stop=(jt == TILES - 1))
                last.then_inc(multiplied[k], 1)

            def attention_rows(k, blk):
                pe.wait_ge(evac_a[k], blk * k + k)
                if k == 1:
                    pe.wait_ge(evac_d[k], blk + 1)
                for it in range(SUB):
                    last = nc.tensor.matmul(ps[4 + it // 3][:, (it % 3) * 130:(it % 3) * 130 + D + 1], hT[:, 0, it * P:(it + 1) * P],
                                            gwd[:, k - 1, :], start=True, stop=True)
                    if it % 3 == 2 or it == SUB - 1:
                        last.then_inc(natural[k], 1)

            attention_top(1)

            def epilogue1(blk, step):
                if step == 1:
                    attention_rows(1, blk)
                if step == 12:
                    turn(1, blk)
                if step == 14:
                    score(1, blk)

            pipelined(pe, lambda blk, jt: attention_stream(1, blk, jt), epilogue1)

            attention_top(2)

            def epilogue2(blk, step):
                if step == 1:
                    attention_rows(2, blk)
                if step == 7:
                    turn(2, blk)
                if step == 9:
                    pe.wait_ge(xT_ready[2], blk * 2 + 2)
                    for it in range(SUB):
                        last = nc.tensor.matmul(ps[4 + it // 3][:, (it % 3) * 130:(it % 3) * 130 + D + 1], xT[:, it * P:(it + 1) * P],
                                                hwt_s[:, :], start=True, stop=True)
                        if it % 3 == 2 or it == SUB - 1:
                            last.then_inc(scores[2], 1)

            pipelined(pe, lambda blk, jt: attention_stream(2, blk, jt), epilogue2)
            pe.wait_ge(hyp_out_d, BLOCKS)
            pe.wait_ge(hyp_out_a, BLOCKS)

            def stream3(blk, jt):
                if jt == 0 and not isinstance(blk, int):
                    pe.wait_ge(evac_a[3], blk * 2)
                split_products(3, blk, jt, ((x_head, x_rest),))

            def epilogue3(blk, step):
                if step == 1:
                    pe.wait_ge(evac_a[3], blk * 2 + 2)
                    for h in range(2):
                        for q in range(4):
                            it = 4 * h + q
                            last = nc.tensor.transpose(ps[4 + h][:, q * P:(q + 1) * P], hT[:, 0, it * P:(it + 1) * P], ident[:, :])
                        last.then_inc(natural[3], 1)

            pipelined(pe, stream3, epilogue3)


def kernel(**inputs):
    import numpy as np
    import concourse.bacc as bacc
    from concourse.bass_utils import run_bass_kernel_spmd

    a = {k: np.asarray(v) for k, v in inputs.items()}

    def rows(v):
        return np.ascontiguousarray(v.reshape(TILES, P, D).transpose(1, 0, 2).reshape(P, N))

    def everywhere(v):
        return np.ascontiguousarray(np.broadcast_to(v.reshape(1, -1), (P, v.size)))

    W1, W2, Wm = a["L0_gnn_W1"], a["L0_gnn_W2"], a["L0_gnn_Wm"]
    gW = [a["L1_gnn_W"], a["L2_gnn_W"]]
    ga = [a["L1_gnn_a"].reshape(2, D), a["L2_gnn_a"].reshape(2, D)]
    arrays = {
        "adj": np.ascontiguousarray(a["adj"].reshape(BLOCKS, BLOCK, TILES, P).transpose(0, 2, 3, 1)).reshape(STREAM * P, BLOCK),
        "x": rows(a["x"]),
        "x2": rows(a["L0_gnn_x2"]),
        "wmlp": np.ascontiguousarray(np.concatenate([w.T for w in W1] + [w.T for w in W2] + [Wm[:, :D].T, Wm[:, D:].T], axis=1)),
        "bmlp": np.ascontiguousarray(np.concatenate([a["L0_gnn_b1"], a["L0_gnn_b2"]]).T),
        "eps": everywhere(np.concatenate([a["L0_gnn_eps1"], a["L0_gnn_eps2"]])),
        "bm": everywhere(a["L0_gnn_bm"]),
        "gw": np.ascontiguousarray(np.concatenate(gW, axis=1)),
        "gwt": np.ascontiguousarray(np.concatenate([w.T for w in gW], axis=1)),
        "glast": np.concatenate([everywhere(w[-1]) for w in gW], axis=1),
        "ga": np.ascontiguousarray(np.concatenate(ga).T),
        "hwt": np.ascontiguousarray(a["L3_gnn_weight"].T),
        "hw": np.ascontiguousarray(a["L3_gnn_weight"]),
        "hbias": everywhere(a["L3_gnn_bias"]),
        "hbcol": a["L3_gnn_bias"].reshape(D, 1),
        "ident": np.eye(P, dtype=np.float32),
    }
    nc = bacc.Bacc("TRN2", target_bir_lowering=False, num_devices=1)
    feed, args = {}, []
    for name, v in arrays.items():
        feed[f"in_{name}"] = v
        args.append(nc.dram_tensor(f"in_{name}", v.shape, mybir.dt.from_np(v.dtype), kind="ExternalInput").ap())
    args.append(nc.dram_tensor("out_rows", (P, N), F32, kind="ExternalOutput").ap())
    build(nc, *args)
    r = run_bass_kernel_spmd(nc, [feed], core_ids=[0])
    got = r.results[0]["out_rows"]
    return np.ascontiguousarray(got.reshape(P, TILES, D).transpose(1, 0, 2)).reshape(N, D)
```

```python
import concourse.bass as bass
from concourse import mybir
from concourse.alu_op_type import AluOpType as ALU
from contextlib import ExitStack
import math

F32 = mybir.dt.float32
F32R = mybir.dt.float32r
U8 = mybir.dt.uint8
ACT = mybir.ActivationFunctionType
AX = mybir.AxisListType

P = 128
D = 128
N = 4096
BLOCK = 1024
BLOCKS = N // BLOCK
TILES = N // P
SUB = BLOCK // P
STREAM = BLOCKS * TILES
HALF = 512
RING = 4
SLOTS3 = 16
READY3 = TILES - SUB
SETUP_D = 15
ROOTS = (1, 1, 3, 2)
LN_EPS = 1e-5
MIN_NORM = 1e-15
MAX_NORM = 1.0 - 1e-5
CLIP = 1.0 - 2.0 ** -23
ATANH_MAX = 0.5 * (math.log1p(MAX_NORM) - math.log1p(-MAX_NORM))


class Chain:

    def __init__(self, eng, sem, per=0):
        self.eng, self.sem, self.per, self.n, self.blk = eng, sem, per, 0, 0

    def block(self, blk):
        self.blk, self.n = blk, 0

    def step(self, ins):
        ins.then_inc(self.sem, 1)
        self.n += 1
        self.eng.wait_ge(self.sem, self.blk * self.per + self.n)

    def end(self):
        assert self.n == self.per, (self.n, self.per)


def pipelined(eng, stream, epilogue, chain=None, before=None, tail=True):
    for jt in range(TILES):
        stream(0, jt)
        if before and jt < READY3:
            for step in range(jt * TILES // READY3, (jt + 1) * TILES // READY3):
                before(step)
    with eng.Fori(1, BLOCKS) as blk:
        if chain:
            chain.block(blk - 1)
        for jt in range(TILES):
            stream(blk, jt)
            epilogue(blk - 1, jt)
        if chain:
            chain.end()
    if chain:
        chain.block(BLOCKS - 1)
    if tail:
        for step in range(TILES):
            epilogue(BLOCKS - 1, step)


def build(nc, adj, x, x2, wmlp, bmlp, eps, bm, gw, gwt, glast, ga, hwt, hw, hbias, hbcol, ident_in, out):
    ctx = ExitStack()
    with ctx:
        def sb(name, shape, dt=F32):
            return ctx.enter_context(nc.sbuf_tensor(name, shape, dt))

        def sem(name):
            return ctx.enter_context(nc.semaphore(name))

        def sems(name, n=RING):
            return [sem(f"{name}{i}") for i in range(n)]

        xn = sb("xn", [P, N])
        x_head = sb("x_head", [P, N], F32R)
        x_rest = sb("x_rest", [P, N], F32R)
        x2_at = nc.sbuf_base
        x2_head = sb("x2_head", [P, N], F32R)
        x2_rest = sb("x2_rest", [P, N], F32R)
        early_adj = nc.alloc_sbuf_tensor_at("early_adj", [P, 2 * N], F32, offset=x2_at)
        xf = sb("xf", [P, N])
        grow = sb("grow", [P, N])
        ring = sb("ring", [P, RING, BLOCK])
        head = sb("head", [P, RING, BLOCK], F32R)
        rest = sb("rest", [P, RING, BLOCK], F32R)
        mask = sb("mask", [P, RING, BLOCK], U8)
        hT = sb("hT", [P, 2, BLOCK])
        xT = sb("xT", [P, BLOCK])
        rows = sb("rows", [P, BLOCK])
        tmp = sb("tmp", [P, BLOCK])
        stats = sb("stats", [P, SUB, 6])
        mv = sb("mv", [P, SUB, 2])
        rstd = sb("rstd", [P, SUB])
        nbias = sb("nbias", [P, SUB])
        den = sb("den", [P, SUB])
        zero = sb("zero", [P, SUB])
        rden = sb("rden", [P, SUB])
        s2 = sb("s2", [P, TILES])
        Hj = sb("Hj", [P, TILES])
        Fj = sb("Fj", [P, TILES])
        xsum = sb("xsum", [P, 2 * BLOCKS])
        small = sb("small", [P, 16])
        sc = sb("sc", [P, 24, SUB])
        wmlp_s = sb("wmlp_s", [P, 8 * D])
        bmlp_s = sb("bmlp_s", [P, 6])
        eps_s = sb("eps_s", [P, 2])
        bm_s = sb("bm_s", [P, D])
        gw_s = sb("gw_s", [P, 2 * D])
        gwt_s = sb("gwt_s", [P, 2 * D])
        glast_s = sb("glast_s", [P, 2 * D])
        ga_s = sb("ga_s", [P, 4])
        hwt_s = sb("hwt_s", [P, D + 1])
        hw_s = sb("hw_s", [P, D])
        hbias_s = sb("hbias_s", [P, D])
        hbcol_s = sb("hbcol_s", [P, 1])
        ident = sb("ident", [P, P])
        ones = sb("ones", [P, P])
        gwd = sb("gwd", [P, 2, D + 1])
        wa = sb("wa", [P, 2, 2])
        wa1 = sb("wa1", [P, 2, P])
        meanwh = sb("meanwh", [P, D])
        diag_ones = sb("diag_ones", [P, SUB], U8)
        halves = sb("halves", [P, 3 * SUB])
        spare = sb("spare", [P, 1])
        bconst = sb("bconst", [P, 4])
        sqs = sb("sqs", [P, D])
        squares = sb("squares", [P, 3, BLOCK], mybir.dt.bfloat16)
        ps = [ctx.enter_context(nc.psum_tensor(f"ps{i}", [P, HALF], F32)) for i in range(8)]
        mask_dram = nc.dram_tensor("mask_scratch", [STREAM * P, BLOCK], U8).ap()

        def slot3(s):
            if s < 2 * RING:
                return early_adj[:, s * BLOCK:(s + 1) * BLOCK]
            q = s % RING
            return grow[:, q * BLOCK:(q + 1) * BLOCK] if s < 3 * RING else ring[:, q, :]

        consts_in = sem("consts_in")
        x_in = sems("x_in_", BLOCKS)
        diag_in = sem("diag_in")
        tile_in = [sems(f"tile_in_{k}_") for k in range(3)]
        tile3_in = sems("tile3_in_", SLOTS3)
        mask_out = sems("mask_out_")
        heads = {k: sem(f"heads_{k}") for k in (0, 3)}
        rests = {k: sem(f"rests_{k}") for k in (0, 3)}
        used = {k: sem(f"used_{k}") for k in (0, 1, 2)}
        root_asked = [sem(f"root_asked_{k}") for k in range(4)]
        root_done = [sem(f"root_done_{k}") for k in range(4)]
        bias_root = sem("bias_root")
        multiplied = [sem(f"multiplied_{k}") for k in range(4)]
        evac_a = [sem(f"evac_a_{k}") for k in range(4)]
        evac_d = {k: sem(f"evac_d_{k}") for k in (0,)}
        mlp_mm = sem("mlp_mm")
        natural = [sem(f"natural_{k}") for k in range(4)]
        rden_ready = sem("rden_ready")
        scaled = sem("scaled")
        relu_done = sem("relu_done")
        rows_read = sem("rows_read")
        norm_ready = {k: sem(f"norm_ready_{k}") for k in (1, 2, 3)}
        rows_done = sem("rows_done")
        rden_ready2 = sem("rden_ready2")
        final_rows = sem("final_rows")
        x_ready = [sem(f"x_ready_{k}") for k in range(4)]
        x_kept = [sem(f"x_kept_{k}") for k in range(3)]
        turned = {k: sem(f"turned_{k}") for k in (0, 1, 2)}
        xT_ready = {k: sem(f"xT_ready_{k}") for k in (0, 1, 2)}
        scores = {k: sem(f"scores_{k}") for k in (0, 1, 2)}
        scored_a = {k: sem(f"scored_a_{k}") for k in (0, 1, 2)}
        scored_d = {k: sem(f"scored_d_{k}") for k in (0, 1)}
        chain_d = [sem(f"chain_d_{k}") for k in range(6)]
        setup_d = sem("setup_d")
        setup_p = sem("setup_p")
        setup_a = sem("setup_a")
        setup_pe = sem("setup_pe")
        split_h = sem("split_h")
        split_r = sem("split_r")
        bm_added = sem("bm_added")
        top_d = {k: sem(f"top_d_{k}") for k in (1, 2)}
        top_pe = {k: sem(f"top_pe_{k}") for k in (1, 2)}
        top_a = {k: sem(f"top_a_{k}") for k in (1, 2)}
        g_ready = {k: sem(f"g_ready_{k}") for k in (1, 2)}
        xf_ready = {k: sem(f"xf_ready_{k}") for k in (1, 2)}
        elu_d = sem("elu_d")
        elu_a = sem("elu_a")
        hyp_d = sem("hyp_d")
        hyp_a = sem("hyp_a")
        hyp_out_a = sem("hyp_out_a")
        hyp_out_d = sem("hyp_out_d")
        fin_d = sem("fin_d")
        fin_a = sem("fin_a")
        stored = sem("stored")
        block = ctx.enter_context(nc.Block())

        def col(buf, blk, it, n=1):
            return buf[:, bass.ds(blk * BLOCK + it * P, n * P)]

        CONSTS = [(wmlp_s, wmlp), (bmlp_s, bmlp), (eps_s, eps), (bm_s, bm), (gw_s, gw), (gwt_s, gwt),
                  (glast_s, glast), (ga_s, ga), (hwt_s, hwt), (hw_s, hw), (hbias_s, hbias),
                  (hbcol_s, hbcol), (ident, ident_in)]

        @block.sync
        def _(sp):
            def tile_rows(buf, t):
                return buf[bass.ds(t * P, P), :]

            def stream(load, between=lambda: None):
                for r in range(RING):
                    load(r, r, True)
                between()
                with sp.Fori(1, STREAM // RING) as g:
                    for r in range(RING):
                        load(g * RING + r, r, False)

            def load_x(c):
                w = slice(c * BLOCK, (c + 1) * BLOCK)
                sp.dma_start(xn[:, w], x[:, w]).then_inc(x_in[c], 16)
                sp.dma_start(grow[:, w], x2[:, w]).then_inc(x_in[c], 16)

            def load0(t, r, first):
                if not first:
                    sp.wait_ge(used[0], t - (RING - 1))
                sp.dma_start(ring[:, r, :], tile_rows(adj, t)).then_inc(tile_in[0][r], 16)
                if not first:
                    sp.dma_start(tile_rows(mask_dram, t - RING), mask[:, r, :]).then_inc(mask_out[r], 16)

            load_x(0)
            for t in range(TILES):
                load0(t, t % RING, t < RING)
                if t == RING - 1:
                    load_x(1)
                if t == SUB - 1:
                    for dst, src in CONSTS:
                        sp.dma_start(dst[:, 0:src.shape[1]], src).then_inc(consts_in, 16)
                if t == 2 * SUB - RING:
                    load_x(2)
                if t == 3 * SUB - RING:
                    load_x(3)
            with sp.Fori(TILES // RING, STREAM // RING) as g:
                for r in range(RING):
                    load0(g * RING + r, r, False)
            for r in range(RING):
                t = STREAM - RING + r
                sp.wait_ge(used[0], t + 1)
                sp.dma_start(tile_rows(mask_dram, t), mask[:, r, :]).then_inc(mask_out[r], 16)
            for r in range(RING):
                sp.wait_ge(mask_out[r], 16 * (STREAM // RING))

            def load_mask(k, t, r, first):
                if not first:
                    sp.wait_ge(used[k], t - (RING - 1))
                elif k == 2:
                    sp.wait_ge(used[1], STREAM - RING + r + 1)
                sp.dma_start(mask[:, r, :], tile_rows(mask_dram, t)).then_inc(tile_in[k][r], 16)

            stream(lambda t, r, first: load_mask(1, t, r, first))
            for r in range(RING):
                sp.wait_ge(tile_in[1][r], 16 * (STREAM // RING))
            for blk in range(BLOCKS):
                t0 = (blk * TILES + blk * SUB) * P
                spot = bass.AP(mask_dram.tensor, t0 * BLOCK, [[BLOCK + 1, P], [P * BLOCK + P, SUB], [1, 1]])
                with nc.allow_non_contiguous_dma(reason="one byte per node"):
                    sp.dma_start(spot, diag_ones[:, :].unsqueeze(2)).then_inc(diag_in, 16)
            sp.wait_ge(diag_in, 16 * BLOCKS)

            def load3(t, s):
                sp.dma_start(slot3(s), tile_rows(adj, t)).then_inc(tile3_in[s], 16)

            def load3_early():
                for s in range(2 * RING):
                    load3(s, s)

            stream(lambda t, r, first: load_mask(2, t, r, first), load3_early)
            for r in range(RING):
                sp.wait_ge(used[2], (r + 1) * TILES)
                load3(2 * RING + r, 2 * RING + r)
            for r in range(RING):
                sp.wait_ge(multiplied[2], STREAM - RING + r + 1)
                load3(3 * RING + r, 3 * RING + r)
            with sp.Fori(1, STREAM // SLOTS3) as g:
                for s in range(SLOTS3):
                    sp.wait_ge(rests[3], g * SLOTS3 + s - (SLOTS3 - 1))
                    load3(g * SLOTS3 + s, s)

            for blk in range(BLOCKS):
                sp.wait_ge(x_ready[3], blk + 1)
                sp.dma_start(out[:, blk * BLOCK:(blk + 1) * BLOCK], xn[:, blk * BLOCK:(blk + 1) * BLOCK]).then_inc(stored, 16)
            sp.wait_ge(stored, 16 * BLOCKS)

        @block.scalar
        def _(act):
            def split_head(k, blk, jt):
                r = jt % RING
                if k == 3:
                    src = slot3(jt % SLOTS3)
                    act.wait_ge(tile3_in[jt % SLOTS3], (blk * (TILES // SLOTS3) + jt // SLOTS3 + 1) * 16)
                else:
                    src = ring[:, r, :]
                    act.wait_ge(tile_in[k][r], (blk * (TILES // RING) + jt // RING + 1) * 16)
                if not (isinstance(blk, int) and blk == 0 and jt < RING):
                    act.wait_ge(multiplied[k], blk * TILES + jt - (RING - 1))
                nc.scalar.activation(head[:, r, :], src, ACT.Copy).then_inc(heads[k], 1)

            def turn_copy(k, blk):
                for h in range(2):
                    act.wait_ge(turned[k], blk * 2 + h + 1)
                    if k == 0:
                        nc.scalar.activation(xT[:, h * HALF:(h + 1) * HALF], ps[4 + h][:, :], ACT.Copy,
                                             accum_out=xsum[:, bass.ds(blk * 2 + h, 1)]).then_inc(xT_ready[k], 1)
                    else:
                        nc.scalar.activation(xT[:, h * HALF:(h + 1) * HALF], ps[4 + h][:, :],
                                             ACT.Copy).then_inc(xT_ready[k], 1)

            def keep_s1(k, blk):
                for h in range(2):
                    act.wait_ge(scores[k], blk * 3 + h + 1)
                    nc.scalar.activation(grow[:, bass.ds(blk * BLOCK + h * HALF, HALF)], ps[6 + h][:, :],
                                         ACT.Copy).then_inc(scored_a[k], 1)

            def split_x(c):
                w = slice(c * BLOCK, (c + 1) * BLOCK)
                act.wait_ge(x_in[c], 32)
                nc.scalar.activation(x_head[:, w], xn[:, w], ACT.Copy).then_inc(split_h, 1)
                nc.scalar.activation(x2_head[:, w], grow[:, w], ACT.Copy).then_inc(split_h, 1)

            def stream0(blk, jt):
                if isinstance(blk, int) and jt % SUB == 0:
                    split_x(jt // SUB)
                split_head(0, blk, jt)
                if isinstance(blk, int) and jt == 2 * SUB:
                    act.wait_ge(bias_root, 1)
                    nc.scalar.activation(bconst[:, 3:4], bconst[:, 2:3], ACT.Tanh).then_inc(setup_a, 1)

            def nothing(blk, step):
                pass

            def epilogue0(blk, step):
                if step == 2:
                    act.wait_ge(setup_d, 4)
                    act.wait_ge(multiplied[0], (blk + 1) * TILES)
                    for h in range(2):
                        nc.scalar.activation(hT[:, 0, h * HALF:(h + 1) * HALF], ps[h][:, :], ACT.Identity,
                                             scale=small[:, 0:1]).then_inc(evac_a[0], 1)
                if 4 <= step < 10:
                    l, h = divmod(step - 4, 2)
                    act.wait_ge(mlp_mm, blk * 12 + 2 * (step - 4) + 1)
                    nc.scalar.activation(hT[:, 0, h * HALF:(h + 1) * HALF], ps[4 + h][:, :], ACT.Relu,
                                         bias=bmlp_s[:, l:l + 1]).then_inc(evac_a[0], 1)
                if step == 18:
                    turn_copy(0, blk)
                if step == 20:
                    keep_s1(0, blk)

            pipelined(act, stream0, epilogue0)

            def attention_tables(k):
                act.wait_ge(top_d[k], 3)
                nc.scalar.activation(Fj[:, :], s2[:, :], ACT.Exp, bias=small[:, 6:7], scale=0.2).then_inc(top_a[k], 1)
                nc.scalar.activation(Hj[:, :], s2[:, :], ACT.Exp, bias=small[:, 5:6], scale=0.8).then_inc(top_a[k], 1)
                for b in range(BLOCKS):
                    act.wait_ge(top_d[k], 4 + b)
                    nc.scalar.activation(grow[:, b * BLOCK:(b + 1) * BLOCK], grow[:, b * BLOCK:(b + 1) * BLOCK],
                                         ACT.Exp, scale=-0.8).then_inc(g_ready[k], 1)

            attention_tables(1)

            def square_sums(src, place, junk, its=range(SUB)):
                for it in its:
                    last = nc.scalar.activation(squares[:, junk, it * P:(it + 1) * P], src[:, it * P:(it + 1) * P], ACT.Square,
                                                accum_out=sc[:, place, it:it + 1])
                return last

            def evacuate(k, blk):
                act.wait_ge(multiplied[k], (blk + 1) * TILES)
                for h in range(2):
                    nc.scalar.activation(hT[:, 0, h * HALF:(h + 1) * HALF], ps[h][:, :], ACT.Copy).then_inc(evac_a[k], 1)

            def apply_norm(k, blk, dst, its=range(SUB)):
                act.wait_ge(norm_ready[k], blk + 1)
                for it in its:
                    last = nc.scalar.activation(dst(it), rows[:, it * P:(it + 1) * P], ACT.Identity,
                                                bias=nbias[:, it:it + 1], scale=rstd[:, it:it + 1])
                if it == SUB - 1:
                    last.then_inc(x_ready[k], 1)

            def keep_rows(k, blk):
                act.wait_ge(x_ready[k], blk + 1)
                nc.scalar.activation(col(xn, blk, 0, SUB), rows[:, :], ACT.Copy).then_inc(x_kept[k], 1)

            def in_place(it):
                return rows[:, it * P:(it + 1) * P]

            def epilogue1(blk, step):
                if step == 2:
                    evacuate(1, blk)
                if step == 5:
                    act.wait_ge(rden_ready, blk + 1)
                    for it in range(SUB):
                        nc.scalar.activation(in_place(it), ps[4 + it // 3][:, (it % 3) * 130:(it % 3) * 130 + D], ACT.Copy,
                                             scale=rden[:, it:it + 1]).then_inc(scaled, 1)
                if step == 8:
                    act.wait_ge(elu_d, blk + 1)
                    nc.scalar.activation(tmp[:, :], tmp[:, :], ACT.Exp).then_inc(elu_a, 1)
                if step == 18:
                    apply_norm(1, blk, in_place)
                if step == 19:
                    keep_rows(1, blk)
                if step == 20:
                    turn_copy(1, blk)
                if step == 22:
                    keep_s1(1, blk)

            pipelined(act, nothing, epilogue1)

            attention_tables(2)

            def epilogue2(blk, step):
                if step == 2:
                    evacuate(2, blk)
                if step == 13:
                    apply_norm(2, blk, in_place)
                if step == 14:
                    keep_rows(2, blk)
                if step == 15:
                    turn_copy(2, blk)
                if step == 16:
                    square_sums(rows, 0, 0).then_inc(hyp_a, 1)
                if step == 17:
                    for b in range(3):
                        n = min(3, SUB - 3 * b)
                        act.wait_ge(scores[2], blk * 3 + b + 1)
                        src = ps[4 + b][:, 0:390].rearrange("p (t c) -> p t c", c=130)
                        nc.scalar.activation(sc[:, 2, 3 * b:3 * b + n], src[:, 0:n, D], ACT.Copy)
                        nc.scalar.activation(tmp[:, 3 * b * P:(3 * b + n) * P].rearrange("p (t c) -> p t c", c=P),
                                             src[:, 0:n, 0:D], ACT.Copy).then_inc(scored_a[2], 1)
                if step == 18:
                    act.wait_ge(scored_a[2], blk * 3 + 3)
                    square_sums(tmp, 1, 1).then_inc(hyp_a, 1)
                if step == 22:
                    act.wait_ge(hyp_d, blk * 6 + 1)
                    nc.scalar.activation(sc[:, 9, :], sc[:, 8, :], ACT.Ln).then_inc(hyp_a, 1)
                if step == 23:
                    act.wait_ge(hyp_d, blk * 6 + 2)
                    nc.scalar.activation(sc[:, 6, :], sc[:, 5, :], ACT.Tanh).then_inc(hyp_a, 1)
                if step == 24:
                    act.wait_ge(hyp_d, blk * 6 + 3)
                    for it in range(SUB):
                        last = nc.scalar.activation(rows[:, it * P:(it + 1) * P], hbias_s[:, :], ACT.Copy, scale=sc[:, 17, it:it + 1])
                    last.then_inc(hyp_a, 1)
                if step == 26:
                    act.wait_ge(hyp_d, blk * 6 + 4)
                    square_sums(tmp, 0, 2).then_inc(hyp_a, 1)
                if step == 30:
                    act.wait_ge(hyp_d, blk * 6 + 5)
                    nc.scalar.activation(sc[:, 9, :], sc[:, 8, :], ACT.Ln).then_inc(hyp_a, 1)
                if step == 31:
                    act.wait_ge(hyp_d, blk * 6 + 6)
                    for it in range(SUB):
                        last = nc.scalar.activation(col(x_head, blk, it), tmp[:, it * P:(it + 1) * P], ACT.Copy,
                                                    scale=sc[:, 16, it:it + 1])
                    last.then_inc(hyp_out_a, 1)

            pipelined(act, nothing, epilogue2, tail=False)

            def epilogue3(blk, step):
                if step == 2:
                    evacuate(3, blk)
                if step == 4:
                    for h in range(2):
                        act.wait_ge(natural[3], blk * 2 + h + 1)
                        nc.scalar.activation(rows[:, h * HALF:(h + 1) * HALF], ps[4 + h][:, :], ACT.Copy).then_inc(rows_read, 1)
                if step in (6, 7):
                    act.wait_ge(rows_read, blk * 2 + 2)
                    last = square_sums(rows, 0, 0, range(4 * (step - 6), 4 * (step - 5)))
                    if step == 7:
                        last.then_inc(fin_a, 1)
                if step in (10, 11):
                    act.wait_ge(relu_done, blk + 1)
                    last = square_sums(tmp, 1, 1, range(4 * (step - 10), 4 * (step - 9)))
                    if step == 11:
                        last.then_inc(fin_a, 1)
                if step == 18:
                    act.wait_ge(fin_d, blk + 1)
                    nc.scalar.activation(sc[:, 5, :], sc[:, 4, :], ACT.Tanh).then_inc(fin_a, 1)
                if 28 <= step < 32:
                    apply_norm(3, blk, lambda it: col(xn, blk, it), range(2 * step - 56, 2 * step - 54))

            pipelined(act, lambda blk, jt: split_head(3, blk, jt), epilogue3,
                      before=lambda step: epilogue2(BLOCKS - 1, step))

        @block.gpsimd
        def _(pool):
            nc.gpsimd.memset(ones[:, :], 1.0).then_inc(setup_p, 1)
            nc.gpsimd.memset(diag_ones[:, :], 1).then_inc(setup_p, 1)
            nc.gpsimd.memset(small[:, :], 0.0).then_inc(setup_p, 1)
            nc.gpsimd.memset(halves[:, 0:2 * SUB], 0.5).then_inc(setup_p, 1)
            nc.gpsimd.memset(halves[:, 2 * SUB:], -0.5).then_inc(setup_p, 1)
            nc.gpsimd.memset(gwd[:, :, :], 0.0).then_inc(setup_p, 1)
            pool.wait_ge(consts_in, 16 * len(CONSTS))
            pool.wait_ge(setup_p, 6)
            pool.wait_ge(setup_d, 3)
            nc.gpsimd.tensor_tensor(bconst[:, 2:3], bconst[:, 2:3], halves[:, 0:1], ALU.pow).then_inc(bias_root, 1)
            pool.wait_ge(split_r, 2 * BLOCKS)
            nc.gpsimd.tensor_tensor(xn[:, :].rearrange("p (t d) -> p t d", d=D), xn[:, :].rearrange("p (t d) -> p t d", d=D),
                                    bm_s[:, :].unsqueeze(1).broadcast_to([P, TILES, D]), ALU.add).then_inc(bm_added, 1)

            def root(k, blk, n, buf, exponent):
                pool.wait_ge(root_asked[k], blk * ROOTS[k] + n)
                nc.gpsimd.tensor_tensor(buf, buf, exponent, ALU.pow).then_inc(root_done[k], 1)

            half, minus_half = halves[:, 0:SUB], halves[:, 2 * SUB:3 * SUB]
            two_halves = halves[:, 0:2 * SUB].rearrange("p (a b) -> p a b", a=2)
            for k in range(2):
                with pool.Fori(0, BLOCKS) as blk:
                    root(k, blk, 1, rstd[:, :], minus_half)

            with pool.Fori(0, BLOCKS) as blk:
                root(2, blk, 1, rstd[:, :], minus_half)
                root(2, blk, 2, sc[:, 3:5, :], two_halves)
                root(2, blk, 3, sc[:, 3, :], half)

            with pool.Fori(0, BLOCKS) as blk:
                pool.wait_ge(rows_read, blk * 2 + 2)
                nc.gpsimd.tensor_tensor(spare[:, :], halves[:, 0:1], halves[:, 0:1], ALU.mult)
                nc.gpsimd.tensor_scalar(tmp[:, :], rows[:, :], 0.0, None, ALU.max).then_inc(relu_done, 1)
                root(3, blk, 1, sc[:, 0:2, :], two_halves)
                root(3, blk, 2, rstd[:, :], minus_half)
        @block.vector
        def _(dve):
            def rest_of(k, blk, jt):
                r = jt % RING
                first = isinstance(blk, int) and jt < RING
                dve.wait_ge(heads[k], blk * TILES + jt + 1)
                if not first:
                    dve.wait_ge(multiplied[k], blk * TILES + jt - (RING - 1))
                src = slot3(jt % SLOTS3) if k == 3 else ring[:, r, :]
                nc.vector.tensor_tensor(rest[:, r, :], src, head[:, r, :].bitcast(F32),
                                        ALU.subtract).then_inc(rests[k], 1)
                if k == 0:
                    if not first:
                        dve.wait_ge(mask_out[r], (blk * (TILES // RING) + jt // RING) * 16)
                    nc.vector.tensor_scalar(mask[:, r, :], ring[:, r, :], 0.0, None, ALU.is_gt).then_inc(used[k], 1)

            def weigh(k, blk, jt):
                r = jt % RING
                dve.wait_ge(tile_in[k][r], (blk * (TILES // RING) + jt // RING + 1) * 16)
                if not (isinstance(blk, int) and jt < RING):
                    dve.wait_ge(multiplied[k], blk * TILES + jt - (RING - 1))
                nc.vector.scalar_tensor_tensor(ring[:, r, :], grow[:, bass.ds(blk * BLOCK, BLOCK)], Hj[:, jt:jt + 1],
                                               mask[:, r, :], ALU.max, ALU.mult).then_inc(used[k], 1)

            def row_stats(ch, its=range(SUB)):
                for it in its:
                    last = nc.vector.bn_stats(stats[:, it, :], rows[:, it * P:(it + 1) * P])
                ch.step(last)

            def deviation(k, ch):
                nc.vector.memset(small[:, 14:15], 0.0)
                for it in range(SUB):
                    last = nc.vector.bn_aggr(mv[:, it, :], stats[:, it, :])
                ch.step(last)
                nc.vector.tensor_scalar(rstd[:, :], mv[:, :, 1], LN_EPS, None, ALU.add).then_inc(root_asked[k], 1)

            def norm_bias(k, blk):
                dve.wait_ge(root_done[k], blk * ROOTS[k] + (2 if k == 3 else 1))
                nc.vector.scalar_tensor_tensor(nbias[:, :], mv[:, :, 0], -1.0, rstd[:, :], ALU.mult, ALU.mult).then_inc(norm_ready[k], 1)

            def normalise(k, blk):
                dve.wait_ge(root_done[k], blk + 1)
                for it in range(SUB):
                    r = rows[:, it * P:(it + 1) * P]
                    last = nc.vector.tensor_scalar(r, r, mv[:, it, 0:1], rstd[:, it:it + 1], ALU.subtract, ALU.mult)
                last.then_inc(x_ready[k], 1)

            def keep_rows(k, blk):
                dve.wait_ge(x_ready[k], blk + 1)
                nc.vector.tensor_scalar(col(xn, blk, 0, SUB), rows[:, :], 1.0, None, ALU.mult).then_inc(x_kept[k], 1)

            def keep_s2(k, blk):
                dve.wait_ge(scores[k], blk * 3 + 3)
                nc.vector.tensor_copy(s2[:, bass.ds(blk * SUB, SUB)], ps[4][:, 0:SUB]).then_inc(scored_d[k], 1)

            def split_x(c):
                w = slice(c * BLOCK, (c + 1) * BLOCK)
                dve.wait_ge(split_h, 2 * c + 1)
                nc.vector.tensor_tensor(x_rest[:, w], xn[:, w], x_head[:, w].bitcast(F32), ALU.subtract).then_inc(split_r, 1)
                dve.wait_ge(split_h, 2 * c + 2)
                nc.vector.tensor_tensor(x2_rest[:, w], grow[:, w], x2_head[:, w].bitcast(F32), ALU.subtract).then_inc(split_r, 1)

            def setup_bias():
                dve.wait_ge(setup_p, 6)
                dve.wait_ge(consts_in, 16 * len(CONSTS))
                nc.vector.tensor_tensor(sqs[:, :], hbias_s[:, :], hbias_s[:, :], ALU.mult).then_inc(setup_d, 1)
                dve.wait_ge(setup_d, 1)
                nc.vector.reduce_sum(bconst[:, 0:1], sqs[:, :], AX.X).then_inc(setup_d, 1)
                dve.wait_ge(setup_d, 2)
                nc.vector.tensor_scalar(bconst[:, 2:3], bconst[:, 0:1], MIN_NORM ** 2, None, ALU.max).then_inc(setup_d, 1)
                nc.vector.tensor_scalar(small[:, 0:2], eps_s[:, :], 2.0, None, ALU.add).then_inc(setup_d, 1)
                dve.wait_ge(setup_d, 4)
            def setup_weights():
                dve.wait_ge(setup_a, 1)
                nc.vector.reciprocal(bconst[:, 2:3], bconst[:, 2:3]).then_inc(setup_d, 1)
                dve.wait_ge(setup_d, 5)
                nc.vector.scalar_tensor_tensor(bconst[:, 1:2], bconst[:, 3:4], MAX_NORM, bconst[:, 2:3], ALU.min, ALU.mult).then_inc(setup_d, 1)
                dve.wait_ge(setup_d, 6)
                nc.vector.scalar_tensor_tensor(bconst[:, 2:3], bconst[:, 1:2], bconst[:, 0:1], bconst[:, 1:2], ALU.mult, ALU.mult).then_inc(setup_d, 1)
                for l in range(2):
                    nc.vector.tensor_tensor(gwd[:, l, 0:D], gw_s[:, l * D:(l + 1) * D], glast_s[:, l * D:(l + 1) * D], ALU.subtract).then_inc(setup_d, 1)
                    nc.vector.tensor_copy(gwd[:, l, D:D + 1], ident[:, P - 1:P]).then_inc(setup_d, 1)
                dve.wait_ge(setup_pe, 1)
                nc.vector.tensor_copy(wa[:, :, :].rearrange("p a b -> p (a b)"), ps[7][:, 0:4]).then_inc(setup_d, 1)
                nc.vector.tensor_copy(hwt_s[:, D:D + 1], ps[7][:, 4:5]).then_inc(setup_d, 1)
                dve.wait_ge(setup_d, 13)
                for l in range(2):
                    nc.vector.tensor_scalar(wa1[:, l, :], ones[:, :], wa[:, l, 0:1], None, ALU.mult).then_inc(setup_d, 1)
                dve.wait_ge(setup_d, SETUP_D)

            ch0 = Chain(dve, chain_d[0], 9)

            def epilogue0(blk, step):
                if step == 2:
                    dve.wait_ge(multiplied[0], (blk + 1) * TILES)
                    for h in range(2):
                        nc.vector.tensor_scalar(hT[:, 1, h * HALF:(h + 1) * HALF], ps[2 + h][:, :], small[:, 1:2], None,
                                                ALU.mult).then_inc(evac_d[0], 1)
                if 4 <= step < 10:
                    l, h = divmod(step - 4, 2)
                    dve.wait_ge(mlp_mm, blk * 12 + 2 * (step - 4) + 2)
                    nc.vector.tensor_scalar(hT[:, 1, h * HALF:(h + 1) * HALF], ps[6 + h][:, :], bmlp_s[:, 3 + l:4 + l],
                                            0.0, ALU.add, ALU.max).then_inc(evac_d[0], 1)
                if step == 11:
                    dve.wait_ge(bm_added, 1)
                if 11 <= step < 15:
                    b = step - 11
                    dve.wait_ge(natural[0], blk * 4 + b + 1)
                    ch0.step(nc.vector.tensor_tensor(rows[:, b * 256:(b + 1) * 256], ps[4 + b][:, 0:256], col(xn, blk, 2 * b, 2), ALU.add))
                    row_stats(ch0, (2 * b, 2 * b + 1))
                if step == 15:
                    deviation(0, ch0)
                if step == 16:
                    normalise(0, blk)
                if step == 17:
                    keep_rows(0, blk)
                if step == 20:
                    keep_s2(0, blk)

            def stream0(blk, jt):
                if isinstance(blk, int) and jt % SUB == 0:
                    split_x(jt // SUB)
                rest_of(0, blk, jt)
                if isinstance(blk, int) and jt == SUB:
                    setup_bias()
                if isinstance(blk, int) and jt == 3 * SUB:
                    setup_weights()

            pipelined(dve, stream0, epilogue0, ch0)

            def attention_top(k):
                dve.wait_ge(scored_d[k - 1], BLOCKS)
                dve.wait_ge(x_kept[k - 1], BLOCKS)
                nc.vector.reduce_max(small[:, 2:3], s2[:, :], AX.X).then_inc(top_d[k], 1)
                dve.wait_ge(top_pe[k], 1)
                nc.vector.reduce_max(small[0:1, 3:4], ps[4][0:1, 0:P], AX.X).then_inc(top_d[k], 1)
                dve.wait_ge(top_pe[k], 2)
                ch = Chain(dve, chain_d[3 + k])
                nc.vector.tensor_copy(small[:, 4:5], ps[5][:, 0:1])
                nc.vector.tensor_scalar(small[:, 6:7], ps[5][:, 0:1], -0.2, None, ALU.mult)
                ch.step(nc.vector.tensor_scalar(small[:, 5:6], ps[5][:, 0:1], -0.8, None, ALU.mult))
                nc.vector.memset(small[:, 14:15], 0.0).then_inc(top_d[k], 1)
                dve.wait_ge(scored_a[k - 1], 2 * BLOCKS)
                for b in range(BLOCKS):
                    nc.vector.tensor_scalar(grow[:, b * BLOCK:(b + 1) * BLOCK], grow[:, b * BLOCK:(b + 1) * BLOCK],
                                            small[:, 4:5], 0.0, ALU.add, ALU.max).then_inc(top_d[k], 1)
                dve.wait_ge(top_a[k], 1)
                for b in range(BLOCKS):
                    xv = xn[:, b * BLOCK:(b + 1) * BLOCK].rearrange("p (t d) -> p t d", d=D)
                    xo = xf[:, b * BLOCK:(b + 1) * BLOCK].rearrange("p (t d) -> p t d", d=D)
                    fv = Fj[:, b * SUB:(b + 1) * SUB].unsqueeze(2)
                    nc.vector.tensor_tensor(xo[:, :, 0:D - 1], xv[:, :, 0:D - 1], fv.broadcast_to([P, SUB, D - 1]), ALU.mult)
                    nc.vector.tensor_copy(xo[:, :, D - 1:D], fv).then_inc(xf_ready[k], 1)
                if k == 1:
                    ch.step(nc.vector.reduce_sum(small[:, 7:8], xsum[:, :], AX.X))
                    nc.vector.tensor_scalar(sqs[:, :], ones[:, :], small[:, 7:8], 1.0 / N, ALU.mult, ALU.mult).then_inc(top_d[k], 1)
                    dve.wait_ge(top_pe[k], 3)
                    nc.vector.tensor_copy(meanwh[:, :], ps[6][:, 0:D]).then_inc(top_d[k], 1)
                dve.wait_ge(top_a[k], 2)

            def denominators(k, blk, done, ch):
                for b in range(3):
                    n = min(3, SUB - 3 * b)
                    dve.wait_ge(natural[k], blk * 3 + b + 1)
                    src = ps[4 + b][:, 0:390].rearrange("p (t c) -> p t c", c=130)[:, 0:n, D]
                    last = nc.vector.tensor_copy(den[:, 3 * b:3 * b + n], src)
                ch.step(last)
                ch.step(nc.vector.tensor_scalar(zero[:, :], den[:, :], 0.0, None, ALU.is_equal))
                ch.step(nc.vector.tensor_tensor(den[:, :], den[:, :], zero[:, :], ALU.add))
                nc.vector.reciprocal(rden[:, :], den[:, :]).then_inc(done, 1)
                dve.wait_ge(done, blk + 1)

            def nat(it):
                return ps[4 + it // 3][:, (it % 3) * 130:(it % 3) * 130 + D]

            attention_top(1)
            ch1 = Chain(dve, chain_d[1], 12)

            def stream1(blk, jt):
                if isinstance(blk, int) and jt == 0:
                    dve.wait_ge(g_ready[1], BLOCKS)
                weigh(1, blk, jt)

            def epilogue1(blk, step):
                if step == 4:
                    denominators(1, blk, rden_ready, ch1)
                if step in (6, 7):
                    for it in range(4 * (step - 6), 4 * (step - 5)):
                        dve.wait_ge(scaled, blk * SUB + it + 1)
                        last = nc.vector.scalar_tensor_tensor(rows[:, it * P:(it + 1) * P], meanwh[:, :], zero[:, it:it + 1],
                                                              rows[:, it * P:(it + 1) * P], ALU.mult, ALU.add)
                    ch1.step(last)
                if step == 8:
                    nc.vector.tensor_scalar(tmp[:, :], rows[:, :], 0.0, None, ALU.min).then_inc(elu_d, 1)
                if step == 9:
                    ch1.step(nc.vector.scalar_tensor_tensor(rows[:, :], rows[:, :], 0.0, col(xn, blk, 0, SUB), ALU.max, ALU.add))
                if step == 11:
                    dve.wait_ge(elu_a, blk + 1)
                    ch1.step(nc.vector.scalar_tensor_tensor(rows[:, :], tmp[:, :], -1.0, rows[:, :], ALU.add, ALU.add))
                if 12 <= step < 16:
                    row_stats(ch1, (2 * step - 24, 2 * step - 23))
                if step == 16:
                    deviation(1, ch1)
                if step == 18:
                    norm_bias(1, blk)
                if step == 26:
                    keep_s2(1, blk)

            pipelined(dve, stream1, epilogue1, ch1)

            attention_top(2)
            ch2 = Chain(dve, chain_d[2], 38)

            def artanh_ln(ch, t):
                ch.step(nc.vector.tensor_scalar(sc[:, 10, :], sc[:, t, :], -1.0, 1.0, ALU.mult, ALU.add))
                ch.step(nc.vector.reciprocal(sc[:, 10, :], sc[:, 10, :]))
                ch.step(nc.vector.scalar_tensor_tensor(sc[:, 7, :], sc[:, t, :], 2.0, sc[:, 10, :], ALU.mult, ALU.mult))
                nc.vector.tensor_scalar(sc[:, 8, :], sc[:, 7, :], 1.0, None, ALU.add).then_inc(hyp_d, 1)

            def artanh_rest(ch, o, asked, ln):
                dve.wait_ge(hyp_d, asked)
                ch.step(nc.vector.tensor_scalar(sc[:, 10, :], sc[:, 8, :], -1.0, None, ALU.add))
                ch.step(nc.vector.tensor_scalar(sc[:, 11, :], sc[:, 10, :], 0.0, None, ALU.is_equal))
                ch.step(nc.vector.tensor_tensor(sc[:, 10, :], sc[:, 10, :], sc[:, 11, :], ALU.add))
                ch.step(nc.vector.reciprocal(sc[:, 10, :], sc[:, 10, :]))
                dve.wait_ge(hyp_a, ln)
                ch.step(nc.vector.tensor_tensor(sc[:, 9, :], sc[:, 9, :], sc[:, 11, :], ALU.add))
                ch.step(nc.vector.tensor_tensor(sc[:, 9, :], sc[:, 9, :], sc[:, 10, :], ALU.mult))
                ch.step(nc.vector.scalar_tensor_tensor(sc[:, o, :], sc[:, 7, :], 0.5, sc[:, 9, :], ALU.mult, ALU.mult))

            def stream2(blk, jt):
                if isinstance(blk, int) and jt == 0:
                    dve.wait_ge(g_ready[2], BLOCKS)
                weigh(2, blk, jt)

            def epilogue2(blk, step):
                if step == 4:
                    denominators(2, blk, rden_ready2, ch2)
                if 5 <= step < 9:
                    for it in (2 * step - 10, 2 * step - 9):
                        last = nc.vector.scalar_tensor_tensor(rows[:, it * P:(it + 1) * P], nat(it), rden[:, it:it + 1],
                                                              col(xn, blk, it), ALU.mult, ALU.add)
                    last.then_inc(rows_done, 1)
                if 6 <= step < 10:
                    dve.wait_ge(rows_done, blk * 4 + step - 5)
                    row_stats(ch2, (2 * step - 12, 2 * step - 11))
                if step == 10:
                    deviation(2, ch2)
                if step == 12:
                    norm_bias(2, blk)
                if step == 19:
                    dve.wait_ge(hyp_a, blk * 7 + 2)
                    nc.vector.tensor_scalar(sc[:, 3:5, :], sc[:, 0:2, :], MIN_NORM ** 2, None, ALU.max).then_inc(root_asked[2], 1)
                if step == 21:
                    dve.wait_ge(root_done[2], blk * 3 + 2)
                    nc.vector.reciprocal(sc[:, 12, :], sc[:, 3, :])
                    nc.vector.reciprocal(sc[:, 13, :], sc[:, 4, :])
                    ch2.step(nc.vector.tensor_scalar(sc[:, 14, :], sc[:, 3, :], CLIP, None, ALU.min))
                    artanh_ln(ch2, 14)
                if step == 22:
                    artanh_rest(ch2, 15, blk * 6 + 1, blk * 7 + 3)
                    ch2.step(nc.vector.tensor_tensor(sc[:, 12, :], sc[:, 4, :], sc[:, 12, :], ALU.mult))
                    nc.vector.tensor_tensor(sc[:, 5, :], sc[:, 12, :], sc[:, 15, :], ALU.mult).then_inc(hyp_d, 1)
                if step == 23:
                    dve.wait_ge(hyp_a, blk * 7 + 4)
                    ch2.step(nc.vector.scalar_tensor_tensor(sc[:, 6, :], sc[:, 6, :], MAX_NORM, sc[:, 13, :], ALU.min, ALU.mult))
                    ch2.step(nc.vector.tensor_tensor(sc[:, 12, :], sc[:, 6, :], sc[:, 6, :], ALU.mult))
                    nc.vector.tensor_tensor(sc[:, 12, :], sc[:, 12, :], sc[:, 1, :], ALU.mult)
                    ch2.step(nc.vector.scalar_tensor_tensor(sc[:, 13, :], sc[:, 2, :], bconst[:, 1:2], sc[:, 6, :], ALU.mult, ALU.mult))
                    ch2.step(nc.vector.tensor_scalar(sc[:, 14, :], sc[:, 13, :], 2.0, 1.0, ALU.mult, ALU.add))
                    nc.vector.scalar_tensor_tensor(sc[:, 15, :], sc[:, 14, :], bconst[:, 2:3], sc[:, 6, :], ALU.add, ALU.mult)
                    nc.vector.tensor_scalar(sc[:, 17, :], sc[:, 12, :], -1.0, 1.0, ALU.mult, ALU.add)
                    ch2.step(nc.vector.scalar_tensor_tensor(sc[:, 18, :], sc[:, 12, :], bconst[:, 2:3], sc[:, 14, :], ALU.mult, ALU.add))
                    ch2.step(nc.vector.tensor_scalar(sc[:, 18, :], sc[:, 18, :], MIN_NORM, None, ALU.max))
                    ch2.step(nc.vector.reciprocal(sc[:, 18, :], sc[:, 18, :]))
                    nc.vector.tensor_tensor(sc[:, 15, :], sc[:, 15, :], sc[:, 18, :], ALU.mult)
                    nc.vector.scalar_tensor_tensor(sc[:, 17, :], sc[:, 17, :], bconst[:, 1:2], sc[:, 18, :], ALU.mult, ALU.mult).then_inc(hyp_d, 1)
                if step == 24:
                    dve.wait_ge(hyp_d, blk * 6 + 3)
                    dve.wait_ge(hyp_a, blk * 7 + 5)
                if step in (24, 25):
                    for it in range(4 * (step - 24), 4 * (step - 23)):
                        t = tmp[:, it * P:(it + 1) * P]
                        last = nc.vector.scalar_tensor_tensor(t, t, sc[:, 15, it:it + 1], rows[:, it * P:(it + 1) * P], ALU.mult, ALU.add)
                if step == 25:
                    last.then_inc(hyp_d, 1)
                if step == 27:
                    dve.wait_ge(hyp_a, blk * 7 + 6)
                    nc.vector.tensor_scalar(sc[:, 3, :], sc[:, 0, :], MIN_NORM ** 2, None, ALU.max).then_inc(root_asked[2], 1)
                if step == 29:
                    dve.wait_ge(root_done[2], blk * 3 + 3)
                    nc.vector.reciprocal(sc[:, 12, :], sc[:, 3, :])
                    ch2.step(nc.vector.tensor_scalar(sc[:, 14, :], sc[:, 3, :], MAX_NORM, None, ALU.min))
                    artanh_ln(ch2, 14)
                if step == 30:
                    artanh_rest(ch2, 15, blk * 6 + 5, blk * 7 + 7)
                    nc.vector.tensor_tensor(sc[:, 16, :], sc[:, 15, :], sc[:, 12, :], ALU.mult).then_inc(hyp_d, 1)
                if step == 31:
                    dve.wait_ge(hyp_d, blk * 6 + 6)
                    dve.wait_ge(hyp_out_a, blk + 1)
                    for it in range(SUB):
                        last = nc.vector.scalar_tensor_tensor(col(x_rest, blk, it), tmp[:, it * P:(it + 1) * P], sc[:, 16, it:it + 1],
                                                              col(x_head, blk, it).bitcast(F32), ALU.mult, ALU.subtract)
                    last.then_inc(hyp_out_d, 1)

            pipelined(dve, stream2, epilogue2, ch2, tail=False)

            ch3 = Chain(dve, chain_d[3], 11)

            def epilogue3(blk, step):
                if step == 13:
                    dve.wait_ge(fin_a, blk * 3 + 2)
                    nc.vector.tensor_scalar(sc[:, 0:2, :], sc[:, 0:2, :], MIN_NORM ** 2, None, ALU.max).then_inc(root_asked[3], 1)
                if step == 16:
                    dve.wait_ge(root_done[3], blk * 2 + 1)
                    ch3.step(nc.vector.reciprocal(sc[:, 3, :], sc[:, 0, :]))
                    ch3.step(nc.vector.scalar_tensor_tensor(sc[:, 2, :], sc[:, 0, :], ATANH_MAX, sc[:, 3, :], ALU.min, ALU.mult))
                    ch3.step(nc.vector.tensor_tensor(sc[:, 4, :], sc[:, 1, :], sc[:, 2, :], ALU.mult))
                    nc.vector.tensor_scalar(sc[:, 4, :], sc[:, 4, :], MIN_NORM, None, ALU.max).then_inc(fin_d, 1)
                if step == 19:
                    dve.wait_ge(fin_d, blk + 1)
                    ch3.step(nc.vector.reciprocal(sc[:, 6, :], sc[:, 4, :]))
                    dve.wait_ge(fin_a, blk * 3 + 3)
                    ch3.step(nc.vector.scalar_tensor_tensor(sc[:, 5, :], sc[:, 5, :], MAX_NORM, sc[:, 6, :], ALU.min, ALU.mult))
                    ch3.step(nc.vector.tensor_tensor(sc[:, 5, :], sc[:, 5, :], sc[:, 2, :], ALU.mult))
                if 21 <= step < 25:
                    for it in (2 * step - 42, 2 * step - 41):
                        last = nc.vector.scalar_tensor_tensor(rows[:, it * P:(it + 1) * P], tmp[:, it * P:(it + 1) * P], sc[:, 5, it:it + 1],
                                                              col(xn, blk, it), ALU.mult, ALU.add)
                    last.then_inc(final_rows, 1)
                if 22 <= step < 26:
                    dve.wait_ge(final_rows, blk * 4 + step - 21)
                    row_stats(ch3, (2 * step - 44, 2 * step - 43))
                if step == 26:
                    deviation(3, ch3)
                if step == 28:
                    norm_bias(3, blk)

            pipelined(dve, lambda blk, jt: rest_of(3, blk, jt), epilogue3, ch3,
                      before=lambda step: epilogue2(BLOCKS - 1, step))

        @block.tensor
        def _(pe):
            def weight_setup():
                pe.wait_ge(consts_in, 16 * len(CONSTS))
                for l in range(2):
                    nc.tensor.matmul(ps[7][:, 2 * l:2 * l + 2], gwt_s[:, l * D:(l + 1) * D], ga_s[:, 2 * l:2 * l + 2], start=True, stop=True)
                nc.tensor.matmul(ps[7][:, 4:5], hw_s[:, :], hbcol_s[:, :], start=True, stop=True).then_inc(setup_pe, 1)

            def split_products(k, blk, jt, operands):
                r = jt % RING
                j = slice(jt * P, (jt + 1) * P)
                pe.wait_ge(heads[k], blk * TILES + jt + 1)
                for n, (xh, xr) in enumerate(operands):
                    if n == 1 and jt == 0 and not isinstance(blk, int):
                        pe.wait_ge(evac_d[k], blk * 8 - 6)
                    for w, st in ((xh, jt == 0), (xr, False)):
                        for h in range(2):
                            nc.tensor.matmul(ps[2 * n + h][:, :], w[:, j], head[:, r, h * HALF:(h + 1) * HALF],
                                             start=st, stop=False)
                pe.wait_ge(rests[k], blk * TILES + jt + 1)
                for n, (xh, xr) in enumerate(operands):
                    for h in range(2):
                        last = nc.tensor.matmul(ps[2 * n + h][:, :], xh[:, j], rest[:, r, h * HALF:(h + 1) * HALF],
                                                start=False, stop=(jt == TILES - 1))
                last.then_inc(multiplied[k], 1)

            def turn(k, blk):
                pe.wait_ge(x_ready[k], blk + 1)
                for h in range(2):
                    for q in range(4):
                        last = nc.tensor.transpose(ps[4 + h][:, q * P:(q + 1) * P], rows[:, (4 * h + q) * P:(4 * h + q + 1) * P], ident[:, :])
                    last.then_inc(turned[k], 1)

            def score(k, blk):
                l = k
                for h in range(2):
                    pe.wait_ge(xT_ready[k], blk * 2 + h + 1)
                    nc.tensor.matmul(ps[6 + h][:, :], wa1[:, l, :], xT[:, h * HALF:(h + 1) * HALF],
                                     start=True, stop=True).then_inc(scores[k], 1)
                for it in range(SUB):
                    last = nc.tensor.matmul(ps[4][:, it:it + 1], xT[:, it * P:(it + 1) * P], wa[:, l, 1:2], start=True, stop=True)
                last.then_inc(scores[k], 1)

            def stream0(blk, jt):
                if jt == 0 and not isinstance(blk, int):
                    pe.wait_ge(evac_a[0], blk * 8 - 6)
                if isinstance(blk, int) and jt % SUB == 0:
                    pe.wait_ge(split_h, jt // SUB * 2 + 2)
                    pe.wait_ge(split_r, jt // SUB * 2 + 2)
                split_products(0, blk, jt, ((x_head, x_rest), (x2_head, x2_rest)))
                if isinstance(blk, int) and jt == SUB:
                    weight_setup()

            def epilogue0(blk, step):
                if 1 <= step < 7:
                    l, h = divmod(step - 1, 2)
                    for n, evac in ((0, evac_a), (1, evac_d)):
                        pe.wait_ge(evac[0], blk * 8 + 2 * l + h + 1)
                        w = (3 * n + l) * D
                        nc.tensor.matmul(ps[4 + 2 * n + h][:, :], wmlp_s[:, w:w + D], hT[:, n, h * HALF:(h + 1) * HALF],
                                         start=True, stop=True).then_inc(mlp_mm, 1)
                if 8 <= step < 12:
                    b = step - 8
                    pe.wait_ge(evac_a[0], blk * 8 + 8)
                    pe.wait_ge(evac_d[0], blk * 8 + 8)
                    for it in (2 * b, 2 * b + 1):
                        for n in range(2):
                            last = nc.tensor.matmul(ps[4 + b][:, (it % 2) * P:(it % 2 + 1) * P], hT[:, n, it * P:(it + 1) * P],
                                                    wmlp_s[:, (6 + n) * D:(7 + n) * D], start=(n == 0), stop=(n == 1))
                    last.then_inc(natural[0], 1)
                if step == 15:
                    turn(0, blk)
                if step == 17:
                    pe.wait_ge(setup_d, SETUP_D)
                    score(0, blk)

            pipelined(pe, stream0, epilogue0)

            def attention_top(k):
                pe.wait_ge(top_d[k], 1)
                pe.wait_ge(scored_a[k - 1], 2 * BLOCKS)
                nc.tensor.transpose(ps[4][0:1, 0:P], small[:, 2:3], ident[:, :]).then_inc(top_pe[k], 1)
                pe.wait_ge(top_d[k], 2)
                nc.tensor.matmul(ps[5][:, 0:1], ones[0:1, :], small[0:1, 3:4], start=True, stop=True).then_inc(top_pe[k], 1)
                if k == 1:
                    pe.wait_ge(top_d[k], 8)
                    nc.tensor.matmul(ps[6][:, 0:D], sqs[:, :], gw_s[:, 0:D], start=True, stop=True).then_inc(top_pe[k], 1)
                    pe.wait_ge(top_d[k], 9)

            def attention_stream(k, blk, jt):
                if jt == 0 and not isinstance(blk, int):
                    pe.wait_ge(evac_a[k], blk * 2)
                if isinstance(blk, int) and jt % SUB == 0:
                    pe.wait_ge(xf_ready[k], jt // SUB + 1)
                pe.wait_ge(used[k], blk * TILES + jt + 1)
                for h in range(2):
                    last = nc.tensor.matmul(ps[h][:, :], xf[:, jt * P:(jt + 1) * P], ring[:, jt % RING, h * HALF:(h + 1) * HALF],
                                            start=(jt == 0), stop=(jt == TILES - 1))
                last.then_inc(multiplied[k], 1)

            def attention_rows(k, blk):
                pe.wait_ge(evac_a[k], blk * 2 + 2)
                for it in range(SUB):
                    last = nc.tensor.matmul(ps[4 + it // 3][:, (it % 3) * 130:(it % 3) * 130 + D + 1], hT[:, 0, it * P:(it + 1) * P],
                                            gwd[:, k - 1, :], start=True, stop=True)
                    if it % 3 == 2 or it == SUB - 1:
                        last.then_inc(natural[k], 1)

            attention_top(1)

            def epilogue1(blk, step):
                if step == 1:
                    attention_rows(1, blk)
                if step == 18:
                    turn(1, blk)
                if step == 21:
                    score(1, blk)

            pipelined(pe, lambda blk, jt: attention_stream(1, blk, jt), epilogue1)

            attention_top(2)

            def epilogue2(blk, step):
                if step == 1:
                    attention_rows(2, blk)
                if step == 12:
                    turn(2, blk)
                if step == 14:
                    pe.wait_ge(xT_ready[2], blk * 2 + 2)
                    for it in range(SUB):
                        last = nc.tensor.matmul(ps[4 + it // 3][:, (it % 3) * 130:(it % 3) * 130 + D + 1], xT[:, it * P:(it + 1) * P],
                                                hwt_s[:, :], start=True, stop=True)
                        if it % 3 == 2 or it == SUB - 1:
                            last.then_inc(scores[2], 1)

            pipelined(pe, lambda blk, jt: attention_stream(2, blk, jt), epilogue2, tail=False)

            def stream3(blk, jt):
                if isinstance(blk, int):
                    if jt == 0:
                        pe.wait_ge(evac_a[2], BLOCKS * 2)
                    if jt % SUB == 0:
                        pe.wait_ge(hyp_out_d, jt // SUB + 1)
                        pe.wait_ge(hyp_out_a, jt // SUB + 1)
                elif jt == 0:
                    pe.wait_ge(evac_a[3], blk * 2)
                split_products(3, blk, jt, ((x_head, x_rest),))

            def epilogue3(blk, step):
                if step == 1:
                    pe.wait_ge(evac_a[3], blk * 2 + 2)
                    for h in range(2):
                        for q in range(4):
                            it = 4 * h + q
                            last = nc.tensor.transpose(ps[4 + h][:, q * P:(q + 1) * P], hT[:, 0, it * P:(it + 1) * P], ident[:, :])
                        last.then_inc(natural[3], 1)

            pipelined(pe, stream3, epilogue3, before=lambda step: epilogue2(BLOCKS - 1, step))


def kernel(**inputs):
    import numpy as np
    import concourse.bacc as bacc
    from concourse.bass_utils import run_bass_kernel_spmd

    a = {k: np.asarray(v) for k, v in inputs.items()}

    def rows(v):
        return np.ascontiguousarray(v.reshape(TILES, P, D).transpose(1, 0, 2).reshape(P, N))

    def everywhere(v):
        return np.ascontiguousarray(np.broadcast_to(v.reshape(1, -1), (P, v.size)))

    W1, W2, Wm = a["L0_gnn_W1"], a["L0_gnn_W2"], a["L0_gnn_Wm"]
    gW = [a["L1_gnn_W"], a["L2_gnn_W"]]
    ga = [a["L1_gnn_a"].reshape(2, D), a["L2_gnn_a"].reshape(2, D)]
    arrays = {
        "adj": np.ascontiguousarray(a["adj"].reshape(BLOCKS, BLOCK, TILES, P).transpose(0, 2, 3, 1)).reshape(STREAM * P, BLOCK),
        "x": rows(a["x"]),
        "x2": rows(a["L0_gnn_x2"]),
        "wmlp": np.ascontiguousarray(np.concatenate([w.T for w in W1] + [w.T for w in W2] + [Wm[:, :D].T, Wm[:, D:].T], axis=1)),
        "bmlp": np.ascontiguousarray(np.concatenate([a["L0_gnn_b1"], a["L0_gnn_b2"]]).T),
        "eps": everywhere(np.concatenate([a["L0_gnn_eps1"], a["L0_gnn_eps2"]])),
        "bm": everywhere(a["L0_gnn_bm"]),
        "gw": np.ascontiguousarray(np.concatenate(gW, axis=1)),
        "gwt": np.ascontiguousarray(np.concatenate([w.T for w in gW], axis=1)),
        "glast": np.concatenate([everywhere(w[-1]) for w in gW], axis=1),
        "ga": np.ascontiguousarray(np.concatenate(ga).T),
        "hwt": np.ascontiguousarray(a["L3_gnn_weight"].T),
        "hw": np.ascontiguousarray(a["L3_gnn_weight"]),
        "hbias": everywhere(a["L3_gnn_bias"]),
        "hbcol": a["L3_gnn_bias"].reshape(D, 1),
        "ident": np.eye(P, dtype=np.float32),
    }
    nc = bacc.Bacc("TRN2", target_bir_lowering=False, num_devices=1)
    feed, args = {}, []
    for name, v in arrays.items():
        feed[f"in_{name}"] = v
        args.append(nc.dram_tensor(f"in_{name}", v.shape, mybir.dt.from_np(v.dtype), kind="ExternalInput").ap())
    args.append(nc.dram_tensor("out_rows", (P, N), F32, kind="ExternalOutput").ap())
    build(nc, *args)
    r = run_bass_kernel_spmd(nc, [feed], core_ids=[0])
    got = r.results[0]["out_rows"]
    return np.ascontiguousarray(got.reshape(P, TILES, D).transpose(1, 0, 2)).reshape(N, D)
```

```python
import concourse.bass as bass
from concourse import mybir
from concourse.alu_op_type import AluOpType as ALU
from contextlib import ExitStack
import math

F32 = mybir.dt.float32
F32R = mybir.dt.float32r
U8 = mybir.dt.uint8
ACT = mybir.ActivationFunctionType
AX = mybir.AxisListType

P = 128
D = 128
N = 4096
BLOCK = 1024
BLOCKS = N // BLOCK
TILES = N // P
SUB = BLOCK // P
STREAM = BLOCKS * TILES
HALF = 512
RING = 4
SLOTS3 = 16
POOL_RESTS = (9, 11, 17, 19, 21, 23)
CARRY = 20
SETUP_D = 15
ROOTS = (1, 1, 3, 2)
LN_EPS = 1e-5
MIN_NORM = 1e-15
MAX_NORM = 1.0 - 1e-5
CLIP = 1.0 - 2.0 ** -23
ATANH_MAX = 0.5 * (math.log1p(MAX_NORM) - math.log1p(-MAX_NORM))


class Chain:

    def __init__(self, eng, sem, per=0):
        self.eng, self.sem, self.per, self.n, self.blk = eng, sem, per, 0, 0

    def block(self, blk):
        self.blk, self.n = blk, 0

    def mark(self, ins):
        ins.then_inc(self.sem, 1)
        self.n += 1

    def step(self, ins):
        self.mark(ins)
        self.wait()

    def wait(self):
        self.eng.wait_ge(self.sem, self.blk * self.per + self.n)

    def end(self):
        assert self.n == self.per, (self.n, self.per)


def pipelined(eng, stream, epilogue, chain=None, before=None, tail=True):
    for jt in range(TILES):
        stream(0, jt)
        if before and jt < CARRY:
            for step in range(jt * TILES // CARRY, (jt + 1) * TILES // CARRY):
                before(step)
    with eng.Fori(1, BLOCKS) as blk:
        if chain:
            chain.block(blk - 1)
        for jt in range(TILES):
            stream(blk, jt)
            epilogue(blk - 1, jt)
        if chain:
            chain.end()
    if chain:
        chain.block(BLOCKS - 1)
    if tail:
        for step in range(TILES):
            epilogue(BLOCKS - 1, step)


def build(nc, adj, x, x2, wmlp, bmlp, eps, bm, gw, gwt, glast, ga, hwt, hw, hbias, hbcol, ident_in, out):
    ctx = ExitStack()
    with ctx:
        def sb(name, shape, dt=F32):
            return ctx.enter_context(nc.sbuf_tensor(name, shape, dt))

        def sem(name):
            return ctx.enter_context(nc.semaphore(name))

        def sems(name, n=RING):
            return [sem(f"{name}{i}") for i in range(n)]

        xn = sb("xn", [P, N])
        x_head = sb("x_head", [P, N], F32R)
        x_rest = sb("x_rest", [P, N], F32R)
        x2_at = nc.sbuf_base
        x2_head = sb("x2_head", [P, N], F32R)
        x2_rest = sb("x2_rest", [P, N], F32R)
        early_adj = nc.alloc_sbuf_tensor_at("early_adj", [P, 2 * N], F32, offset=x2_at)
        xf = sb("xf", [P, N])
        grow = sb("grow", [P, N])
        ring = sb("ring", [P, RING, BLOCK])
        head = sb("head", [P, RING, BLOCK], F32R)
        rest = sb("rest", [P, RING, BLOCK], F32R)
        mask = sb("mask", [P, RING, BLOCK], U8)
        hT = sb("hT", [P, 2, BLOCK])
        xT = sb("xT", [P, BLOCK])
        rows = sb("rows", [P, BLOCK])
        tmp = sb("tmp", [P, BLOCK])
        stats = sb("stats", [P, SUB, 6])
        mv = sb("mv", [P, SUB, 2])
        rstd = sb("rstd", [P, SUB])
        nbias = sb("nbias", [P, SUB])
        den = sb("den", [P, SUB])
        zero = sb("zero", [P, SUB])
        rden = sb("rden", [P, SUB])
        s2 = sb("s2", [P, TILES])
        Hj = sb("Hj", [P, TILES])
        Fj = sb("Fj", [P, TILES])
        xsum = sb("xsum", [P, 2 * BLOCKS])
        small = sb("small", [P, 16])
        sc = sb("sc", [P, 24, SUB])
        wmlp_s = sb("wmlp_s", [P, 8 * D])
        bmlp_s = sb("bmlp_s", [P, 6])
        eps_s = sb("eps_s", [P, 2])
        bm_s = sb("bm_s", [P, D])
        gw_s = sb("gw_s", [P, 2 * D])
        gwt_s = sb("gwt_s", [P, 2 * D])
        glast_s = sb("glast_s", [P, 2 * D])
        ga_s = sb("ga_s", [P, 4])
        hwt_s = sb("hwt_s", [P, D + 1])
        hw_s = sb("hw_s", [P, D])
        hbias_s = sb("hbias_s", [P, D])
        hbcol_s = sb("hbcol_s", [P, 1])
        ident = sb("ident", [P, P])
        ones = sb("ones", [P, P])
        gwd = sb("gwd", [P, 2, D + 1])
        wa = sb("wa", [P, 2, 2])
        wa1 = sb("wa1", [P, 2, P])
        meanwh = sb("meanwh", [P, D])
        diag_ones = sb("diag_ones", [P, SUB], U8)
        halves = sb("halves", [P, 3 * SUB])
        spare = sb("spare", [P, 1])
        bconst = sb("bconst", [P, 4])
        sqs = sb("sqs", [P, D])
        squares = sb("squares", [P, 3, BLOCK], mybir.dt.bfloat16)
        ps = [ctx.enter_context(nc.psum_tensor(f"ps{i}", [P, HALF], F32)) for i in range(8)]
        mask_dram = nc.dram_tensor("mask_scratch", [STREAM * P, BLOCK], U8).ap()

        def slot3(s):
            if s < 2 * RING:
                return early_adj[:, s * BLOCK:(s + 1) * BLOCK]
            q = s % RING
            return grow[:, q * BLOCK:(q + 1) * BLOCK] if s < 3 * RING else ring[:, q, :]

        consts_in = sem("consts_in")
        x_in = sems("x_in_", BLOCKS)
        diag_in = sem("diag_in")
        tile_in = [sems(f"tile_in_{k}_") for k in range(3)]
        tile3_in = sems("tile3_in_", SLOTS3)
        mask_out = sems("mask_out_")
        heads = {k: sem(f"heads_{k}") for k in (0, 3)}
        rests = {k: sem(f"rests_{k}") for k in (0, 3)}
        used = {k: sem(f"used_{k}") for k in (0, 1, 2)}
        root_asked = [sem(f"root_asked_{k}") for k in range(4)]
        root_done = [sem(f"root_done_{k}") for k in range(4)]
        bias_root = sem("bias_root")
        multiplied = [sem(f"multiplied_{k}") for k in range(4)]
        evac_a = [sem(f"evac_a_{k}") for k in range(4)]
        evac_d = {k: sem(f"evac_d_{k}") for k in (0,)}
        mlp_mm = sem("mlp_mm")
        natural = [sem(f"natural_{k}") for k in range(4)]
        rden_ready = sem("rden_ready")
        scaled = sem("scaled")
        relu_done = sem("relu_done")
        rows_read = sem("rows_read")
        norm_ready = {k: sem(f"norm_ready_{k}") for k in (1, 2, 3)}
        rows_done = sem("rows_done")
        rden_ready2 = sem("rden_ready2")
        final_rows = sem("final_rows")
        x_ready = [sem(f"x_ready_{k}") for k in range(4)]
        x_kept = [sem(f"x_kept_{k}") for k in range(3)]
        turned = {k: sem(f"turned_{k}") for k in (0, 1, 2)}
        xT_ready = {k: sem(f"xT_ready_{k}") for k in (0, 1, 2)}
        scores = {k: sem(f"scores_{k}") for k in (0, 1, 2)}
        scored_a = {k: sem(f"scored_a_{k}") for k in (0, 1, 2)}
        scored_d = {k: sem(f"scored_d_{k}") for k in (0, 1)}
        chain_d = [sem(f"chain_d_{k}") for k in range(6)]
        setup_d = sem("setup_d")
        setup_p = sem("setup_p")
        setup_a = sem("setup_a")
        setup_pe = sem("setup_pe")
        split_h = sem("split_h")
        split_r = sem("split_r")
        bm_added = sem("bm_added")
        top_d = {k: sem(f"top_d_{k}") for k in (1, 2)}
        top_pe = {k: sem(f"top_pe_{k}") for k in (1, 2)}
        top_a = {k: sem(f"top_a_{k}") for k in (1, 2)}
        g_ready = {k: sem(f"g_ready_{k}") for k in (1, 2)}
        xf_ready = {k: sem(f"xf_ready_{k}") for k in (1, 2)}
        pool_rests = sem("pool_rests")
        bank_done = [sem(f"bank_done_{k}") for k in range(4)]
        mean_d = sem("mean_d")
        mean_pe = sem("mean_pe")
        elu_d = sem("elu_d")
        elu_a = sem("elu_a")
        hyp_d = sem("hyp_d")
        hyp_a = sem("hyp_a")
        hyp_out_a = sem("hyp_out_a")
        hyp_out_d = sem("hyp_out_d")
        fin_d = sem("fin_d")
        fin_a = sem("fin_a")
        stored = sem("stored")
        block = ctx.enter_context(nc.Block())

        def col(buf, blk, it, n=1):
            return buf[:, bass.ds(blk * BLOCK + it * P, n * P)]

        CONSTS = [(wmlp_s, wmlp), (bmlp_s, bmlp), (eps_s, eps), (bm_s, bm), (gw_s, gw), (gwt_s, gwt),
                  (glast_s, glast), (ga_s, ga), (hwt_s, hwt), (hw_s, hw), (hbias_s, hbias),
                  (hbcol_s, hbcol), (ident, ident_in)]

        @block.sync
        def _(sp):
            def tile_rows(buf, t):
                return buf[bass.ds(t * P, P), :]

            def stream(load, between=lambda: None):
                for r in range(RING):
                    load(r, r, True)
                between()
                with sp.Fori(1, STREAM // RING) as g:
                    for r in range(RING):
                        load(g * RING + r, r, False)

            def load_x(c):
                w = slice(c * BLOCK, (c + 1) * BLOCK)
                sp.dma_start(xn[:, w], x[:, w]).then_inc(x_in[c], 16)
                sp.dma_start(grow[:, w], x2[:, w]).then_inc(x_in[c], 16)

            def load0(t, r, first):
                if not first:
                    sp.wait_ge(used[0], t - (RING - 1))
                sp.dma_start(ring[:, r, :], tile_rows(adj, t)).then_inc(tile_in[0][r], 16)
                if not first:
                    sp.dma_start(tile_rows(mask_dram, t - RING), mask[:, r, :]).then_inc(mask_out[r], 16)

            load_x(0)
            for t in range(TILES):
                load0(t, t % RING, t < RING)
                if t == RING - 1:
                    load_x(1)
                if t == SUB - 1:
                    for dst, src in CONSTS:
                        sp.dma_start(dst[:, 0:src.shape[1]], src).then_inc(consts_in, 16)
                if t == 2 * SUB - RING:
                    load_x(2)
                if t == 3 * SUB - RING:
                    load_x(3)
            with sp.Fori(TILES // RING, STREAM // RING) as g:
                for r in range(RING):
                    load0(g * RING + r, r, False)
            for r in range(RING):
                t = STREAM - RING + r
                sp.wait_ge(used[0], t + 1)
                sp.dma_start(tile_rows(mask_dram, t), mask[:, r, :]).then_inc(mask_out[r], 16)
            for r in range(RING):
                sp.wait_ge(mask_out[r], 16 * (STREAM // RING))

            def load_mask(k, t, r, first):
                if not first:
                    sp.wait_ge(used[k], t - (RING - 1))
                elif k == 2:
                    sp.wait_ge(used[1], STREAM - RING + r + 1)
                sp.dma_start(mask[:, r, :], tile_rows(mask_dram, t)).then_inc(tile_in[k][r], 16)

            stream(lambda t, r, first: load_mask(1, t, r, first))
            for r in range(RING):
                sp.wait_ge(tile_in[1][r], 16 * (STREAM // RING))
            for blk in range(BLOCKS):
                t0 = (blk * TILES + blk * SUB) * P
                spot = bass.AP(mask_dram.tensor, t0 * BLOCK, [[BLOCK + 1, P], [P * BLOCK + P, SUB], [1, 1]])
                with nc.allow_non_contiguous_dma(reason="one byte per node"):
                    sp.dma_start(spot, diag_ones[:, :].unsqueeze(2)).then_inc(diag_in, 16)
            sp.wait_ge(diag_in, 16 * BLOCKS)

            def load3(t, s):
                sp.dma_start(slot3(s), tile_rows(adj, t)).then_inc(tile3_in[s], 16)

            def load3_early():
                for s in range(2 * RING):
                    load3(s, s)

            stream(lambda t, r, first: load_mask(2, t, r, first), load3_early)
            for r in range(RING):
                sp.wait_ge(used[2], (r + 1) * TILES)
                load3(2 * RING + r, 2 * RING + r)
            for r in range(RING):
                sp.wait_ge(multiplied[2], STREAM - RING + r + 1)
                load3(3 * RING + r, 3 * RING + r)
            with sp.Fori(1, STREAM // SLOTS3) as g:
                for s in range(SLOTS3):
                    sp.wait_ge(multiplied[3], g * SLOTS3 + s - (SLOTS3 - 1))
                    load3(g * SLOTS3 + s, s)

            for half in range(2 * BLOCKS):
                w = slice(half * HALF, (half + 1) * HALF)
                sp.wait_ge(x_ready[3], half + 1)
                sp.dma_start(out[:, w], xn[:, w]).then_inc(stored, 16)
            sp.wait_ge(stored, 16 * 2 * BLOCKS)

        @block.scalar
        def _(act):
            def split_head(k, blk, jt):
                r = jt % RING
                if k == 3:
                    src = slot3(jt % SLOTS3)
                    act.wait_ge(tile3_in[jt % SLOTS3], (blk * (TILES // SLOTS3) + jt // SLOTS3 + 1) * 16)
                else:
                    src = ring[:, r, :]
                    act.wait_ge(tile_in[k][r], (blk * (TILES // RING) + jt // RING + 1) * 16)
                if not (isinstance(blk, int) and blk == 0 and jt < RING):
                    act.wait_ge(multiplied[k], blk * TILES + jt - (RING - 1))
                nc.scalar.activation(head[:, r, :], src, ACT.Copy).then_inc(heads[k], 1)

            def turn_copy(k, blk):
                for h in range(2):
                    act.wait_ge(turned[k], blk * 2 + h + 1)
                    if k == 0:
                        nc.scalar.activation(xT[:, h * HALF:(h + 1) * HALF], ps[4 + h][:, :], ACT.Copy,
                                             accum_out=xsum[:, bass.ds(blk * 2 + h, 1)]).then_inc(xT_ready[k], 1)
                    else:
                        nc.scalar.activation(xT[:, h * HALF:(h + 1) * HALF], ps[4 + h][:, :],
                                             ACT.Copy).then_inc(xT_ready[k], 1)

            def keep_s1(k, blk):
                for h in range(2):
                    act.wait_ge(scores[k], blk * 3 + h + 1)
                    nc.scalar.activation(grow[:, bass.ds(blk * BLOCK + h * HALF, HALF)], ps[6 + h][:, :],
                                         ACT.Copy).then_inc(scored_a[k], 1)

            def split_x(c):
                w = slice(c * BLOCK, (c + 1) * BLOCK)
                act.wait_ge(x_in[c], 32)
                nc.scalar.activation(x_head[:, w], xn[:, w], ACT.Copy).then_inc(split_h, 1)
                nc.scalar.activation(x2_head[:, w], grow[:, w], ACT.Copy).then_inc(split_h, 1)

            def stream0(blk, jt):
                if isinstance(blk, int) and jt % SUB == 0:
                    split_x(jt // SUB)
                split_head(0, blk, jt)
                if isinstance(blk, int) and jt == 2 * SUB:
                    act.wait_ge(bias_root, 1)
                    nc.scalar.activation(bconst[:, 3:4], bconst[:, 2:3], ACT.Tanh).then_inc(setup_a, 1)

            def nothing(blk, jt):
                pass

            def epilogue0(blk, step):
                if step == 2:
                    act.wait_ge(setup_d, 4)
                    for h in range(2):
                        act.wait_ge(bank_done[0], blk * 3 + h + 1)
                        nc.scalar.activation(hT[:, 0, h * HALF:(h + 1) * HALF], ps[h][:, :], ACT.Identity,
                                             scale=small[:, 0:1]).then_inc(evac_a[0], 1)
                if 4 <= step < 10:
                    l, h = divmod(step - 4, 2)
                    act.wait_ge(mlp_mm, blk * 12 + 2 * (step - 4) + 1)
                    nc.scalar.activation(hT[:, 0, h * HALF:(h + 1) * HALF], ps[4 + h][:, :], ACT.Relu,
                                         bias=bmlp_s[:, l:l + 1]).then_inc(evac_a[0], 1)
                if step == 18:
                    turn_copy(0, blk)
                if step == 20:
                    keep_s1(0, blk)

            pipelined(act, stream0, epilogue0)

            def attention_tables(k):
                act.wait_ge(top_d[k], 3)
                nc.scalar.activation(Fj[:, :], s2[:, :], ACT.Exp, bias=small[:, 6:7], scale=0.2).then_inc(top_a[k], 1)
                nc.scalar.activation(Hj[:, :], s2[:, :], ACT.Exp, bias=small[:, 5:6], scale=0.8).then_inc(top_a[k], 1)
                for b in range(BLOCKS):
                    act.wait_ge(top_d[k], 4 + b)
                    nc.scalar.activation(grow[:, b * BLOCK:(b + 1) * BLOCK], grow[:, b * BLOCK:(b + 1) * BLOCK],
                                         ACT.Exp, scale=-0.8).then_inc(g_ready[k], 1)

            attention_tables(1)

            def square_sums(src, place, junk, its=range(SUB)):
                for it in its:
                    last = nc.scalar.activation(squares[:, junk, it * P:(it + 1) * P], src[:, it * P:(it + 1) * P], ACT.Square,
                                                accum_out=sc[:, place, it:it + 1])
                return last

            def evacuate(k, blk):
                for h in range(2):
                    if h == 0:
                        act.wait_ge(bank_done[k], blk + 1)
                    else:
                        act.wait_ge(multiplied[k], (blk + 1) * TILES)
                    nc.scalar.activation(hT[:, 0, h * HALF:(h + 1) * HALF], ps[h][:, :], ACT.Copy).then_inc(evac_a[k], 1)

            def apply_norm(k, blk, dst, its=range(SUB)):
                act.wait_ge(norm_ready[k], blk + 1)
                for it in its:
                    last = nc.scalar.activation(dst(it), rows[:, it * P:(it + 1) * P], ACT.Identity,
                                                bias=nbias[:, it:it + 1], scale=rstd[:, it:it + 1])
                    if it % 4 == 3:
                        last.then_inc(x_ready[k], 1)

            def keep_rows(k, blk):
                act.wait_ge(x_ready[k], blk * 2 + 2)
                nc.scalar.activation(col(xn, blk, 0, SUB), rows[:, :], ACT.Copy).then_inc(x_kept[k], 1)

            def in_place(it):
                return rows[:, it * P:(it + 1) * P]

            def epilogue1(blk, step):
                if step == 2:
                    evacuate(1, blk)
                if step == 5:
                    act.wait_ge(rden_ready, blk + 1)
                    for it in range(SUB):
                        nc.scalar.activation(in_place(it), ps[4 + it // 3][:, (it % 3) * 130:(it % 3) * 130 + D], ACT.Copy,
                                             scale=rden[:, it:it + 1]).then_inc(scaled, 1)
                if step == 8:
                    act.wait_ge(elu_d, blk + 1)
                    nc.scalar.activation(tmp[:, :], tmp[:, :], ACT.Exp).then_inc(elu_a, 1)
                if step == 18:
                    apply_norm(1, blk, in_place)
                if step == 20:
                    turn_copy(1, blk)
                if step == 21:
                    keep_rows(1, blk)
                if step == 22:
                    keep_s1(1, blk)

            pipelined(act, nothing, epilogue1)

            attention_tables(2)

            def epilogue2(blk, step):
                if step == 2:
                    evacuate(2, blk)
                if step == 12:
                    apply_norm(2, blk, in_place)
                if step == 14:
                    turn_copy(2, blk)
                if step == 16:
                    for b in range(3):
                        n = min(3, SUB - 3 * b)
                        act.wait_ge(scores[2], blk * 3 + b + 1)
                        src = ps[4 + b][:, 0:390].rearrange("p (t c) -> p t c", c=130)
                        nc.scalar.activation(sc[:, 2, 3 * b:3 * b + n], src[:, 0:n, D], ACT.Copy)
                        nc.scalar.activation(tmp[:, 3 * b * P:(3 * b + n) * P].rearrange("p (t c) -> p t c", c=P),
                                             src[:, 0:n, 0:D], ACT.Copy).then_inc(scored_a[2], 1)
                if step == 17:
                    act.wait_ge(scored_a[2], blk * 3 + 3)
                    square_sums(tmp, 1, 1).then_inc(hyp_a, 1)
                if step == 19:
                    keep_rows(2, blk)
                if step == 21:
                    act.wait_ge(hyp_d, blk * 6 + 1)
                    nc.scalar.activation(sc[:, 9, :], sc[:, 8, :], ACT.Ln).then_inc(hyp_a, 1)
                if step == 22:
                    act.wait_ge(hyp_d, blk * 6 + 2)
                    nc.scalar.activation(sc[:, 6, :], sc[:, 5, :], ACT.Tanh).then_inc(hyp_a, 1)
                if step == 23:
                    act.wait_ge(hyp_d, blk * 6 + 3)
                    for it in range(SUB):
                        last = nc.scalar.activation(rows[:, it * P:(it + 1) * P], hbias_s[:, :], ACT.Copy, scale=sc[:, 17, it:it + 1])
                    last.then_inc(hyp_a, 1)
                if step == 25:
                    act.wait_ge(hyp_d, blk * 6 + 4)
                    square_sums(tmp, 0, 2).then_inc(hyp_a, 1)
                if step == 29:
                    act.wait_ge(hyp_d, blk * 6 + 5)
                    nc.scalar.activation(sc[:, 9, :], sc[:, 8, :], ACT.Ln).then_inc(hyp_a, 1)
                if step == 30:
                    act.wait_ge(hyp_d, blk * 6 + 6)
                    for it in range(SUB):
                        last = nc.scalar.activation(col(x_head, blk, it), tmp[:, it * P:(it + 1) * P], ACT.Copy,
                                                    scale=sc[:, 16, it:it + 1])
                        if it % 4 == 3:
                            last.then_inc(hyp_out_a, 1)

            pipelined(act, nothing, epilogue2, tail=False)

            def epilogue3(blk, step):
                if step == 0:
                    evacuate(3, blk)
                if step == 4:
                    for h in range(2):
                        act.wait_ge(natural[3], blk * 2 + h + 1)
                        nc.scalar.activation(rows[:, h * HALF:(h + 1) * HALF], ps[4 + h][:, :], ACT.Copy).then_inc(rows_read, 1)
                if step in (6, 7):
                    act.wait_ge(rows_read, blk * 2 + 2)
                    last = square_sums(rows, 0, 0, range(4 * (step - 6), 4 * (step - 5)))
                    if step == 7:
                        last.then_inc(fin_a, 1)
                if step in (10, 11):
                    act.wait_ge(relu_done, blk + 1)
                    last = square_sums(tmp, 1, 1, range(4 * (step - 10), 4 * (step - 9)))
                    if step == 11:
                        last.then_inc(fin_a, 1)
                if step == 17:
                    act.wait_ge(fin_d, blk + 1)
                    nc.scalar.activation(sc[:, 5, :], sc[:, 4, :], ACT.Tanh).then_inc(fin_a, 1)
                if 28 <= step < 32:
                    apply_norm(3, blk, lambda it: col(xn, blk, it), range(2 * step - 56, 2 * step - 54))

            pipelined(act, lambda blk, jt: split_head(3, blk, jt), epilogue3,
                      before=lambda step: epilogue2(BLOCKS - 1, step))

        @block.gpsimd
        def _(pool):
            nc.gpsimd.memset(ones[:, :], 1.0).then_inc(setup_p, 1)
            nc.gpsimd.memset(diag_ones[:, :], 1).then_inc(setup_p, 1)
            nc.gpsimd.memset(small[:, :], 0.0).then_inc(setup_p, 1)
            nc.gpsimd.memset(halves[:, 0:2 * SUB], 0.5).then_inc(setup_p, 1)
            nc.gpsimd.memset(halves[:, 2 * SUB:], -0.5).then_inc(setup_p, 1)
            nc.gpsimd.memset(gwd[:, :, :], 0.0).then_inc(setup_p, 1)
            pool.wait_ge(consts_in, 16 * len(CONSTS))
            pool.wait_ge(setup_p, 6)
            pool.wait_ge(setup_d, 3)
            nc.gpsimd.tensor_tensor(bconst[:, 2:3], bconst[:, 2:3], halves[:, 0:1], ALU.pow).then_inc(bias_root, 1)
            pool.wait_ge(split_r, 2 * BLOCKS)
            nc.gpsimd.tensor_tensor(xn[:, :].rearrange("p (t d) -> p t d", d=D), xn[:, :].rearrange("p (t d) -> p t d", d=D),
                                    bm_s[:, :].unsqueeze(1).broadcast_to([P, TILES, D]), ALU.add).then_inc(bm_added, 1)

            def root(k, blk, n, buf, exponent):
                pool.wait_ge(root_asked[k], blk * ROOTS[k] + n)
                nc.gpsimd.tensor_tensor(buf, buf, exponent, ALU.pow).then_inc(root_done[k], 1)

            half, minus_half = halves[:, 0:SUB], halves[:, 2 * SUB:3 * SUB]
            two_halves = halves[:, 0:2 * SUB].rearrange("p (a b) -> p a b", a=2)
            for k in range(2):
                with pool.Fori(0, BLOCKS) as blk:
                    root(k, blk, 1, rstd[:, :], minus_half)

            with pool.Fori(0, BLOCKS) as blk:
                root(2, blk, 1, rstd[:, :], minus_half)
                root(2, blk, 2, sc[:, 3:5, :], two_halves)
                root(2, blk, 3, sc[:, 3, :], half)

            def relu_rows(blk):
                pool.wait_ge(rows_read, blk * 2 + 2)
                nc.gpsimd.tensor_tensor(spare[:, :], halves[:, 0:1], halves[:, 0:1], ALU.mult)
                nc.gpsimd.tensor_scalar(tmp[:, :], rows[:, :], 0.0, None, ALU.max).then_inc(relu_done, 1)

            def pool_rest(blk, jt):
                r = jt % RING
                pool.wait_ge(multiplied[3], blk * TILES + jt - (RING - 1))
                pool.wait_ge(heads[3], blk * TILES + jt + 1)
                nc.gpsimd.tensor_tensor(rest[:, r, :], slot3(jt % SLOTS3), head[:, r, :].bitcast(F32),
                                        ALU.subtract).then_inc(pool_rests, 1)

            def epilogue3(blk, stream_blk):
                if stream_blk is not None:
                    relu_rows(blk)
                for jt in POOL_RESTS[:2] if stream_blk is not None else ():
                    pool_rest(stream_blk, jt)
                root(3, blk, 1, sc[:, 0:2, :], two_halves)
                for jt in POOL_RESTS[2:] if stream_blk is not None else ():
                    pool_rest(stream_blk, jt)
                root(3, blk, 2, rstd[:, :], minus_half)

            with pool.Fori(1, BLOCKS) as blk:
                epilogue3(blk - 1, blk)
            epilogue3(BLOCKS - 1, None)

        @block.vector
        def _(dve):
            def rest_of(k, blk, jt):
                r = jt % RING
                first = isinstance(blk, int) and jt < RING
                if k == 3 and not isinstance(blk, int) and jt in POOL_RESTS:
                    return
                dve.wait_ge(heads[k], blk * TILES + jt + 1)
                if not first:
                    dve.wait_ge(multiplied[k], blk * TILES + jt - (RING - 1))
                src = slot3(jt % SLOTS3) if k == 3 else ring[:, r, :]
                nc.vector.tensor_tensor(rest[:, r, :], src, head[:, r, :].bitcast(F32),
                                        ALU.subtract).then_inc(rests[k], 1)
                if k == 0:
                    if not first:
                        dve.wait_ge(mask_out[r], (blk * (TILES // RING) + jt // RING) * 16)
                    nc.vector.tensor_scalar(mask[:, r, :], ring[:, r, :], 0.0, None, ALU.is_gt).then_inc(used[k], 1)

            def weigh(k, blk, jt):
                r = jt % RING
                dve.wait_ge(tile_in[k][r], (blk * (TILES // RING) + jt // RING + 1) * 16)
                if not (isinstance(blk, int) and jt < RING):
                    dve.wait_ge(multiplied[k], blk * TILES + jt - (RING - 1))
                nc.vector.scalar_tensor_tensor(ring[:, r, :], grow[:, bass.ds(blk * BLOCK, BLOCK)], Hj[:, jt:jt + 1],
                                               mask[:, r, :], ALU.max, ALU.mult).then_inc(used[k], 1)

            def row_stats(ch, its=range(SUB)):
                for it in its:
                    last = nc.vector.bn_stats(stats[:, it, :], rows[:, it * P:(it + 1) * P])
                ch.mark(last)

            def deviation(k, ch):
                ch.wait()
                nc.vector.memset(small[:, 14:15], 0.0)
                for it in range(SUB):
                    last = nc.vector.bn_aggr(mv[:, it, :], stats[:, it, :])
                ch.step(last)
                nc.vector.tensor_scalar(rstd[:, :], mv[:, :, 1], LN_EPS, None, ALU.add).then_inc(root_asked[k], 1)

            def norm_bias(k, blk):
                dve.wait_ge(root_done[k], blk * ROOTS[k] + (2 if k == 3 else 1))
                nc.vector.scalar_tensor_tensor(nbias[:, :], mv[:, :, 0], -1.0, rstd[:, :], ALU.mult, ALU.mult).then_inc(norm_ready[k], 1)

            def normalise(k, blk):
                dve.wait_ge(root_done[k], blk + 1)
                for it in range(SUB):
                    r = rows[:, it * P:(it + 1) * P]
                    last = nc.vector.tensor_scalar(r, r, mv[:, it, 0:1], rstd[:, it:it + 1], ALU.subtract, ALU.mult)
                    if it % 4 == 3:
                        last.then_inc(x_ready[k], 1)

            def keep_rows(k, blk):
                dve.wait_ge(x_ready[k], blk * 2 + 2)
                nc.vector.tensor_scalar(col(xn, blk, 0, SUB), rows[:, :], 1.0, None, ALU.mult).then_inc(x_kept[k], 1)

            def keep_s2(k, blk):
                dve.wait_ge(scores[k], blk * 3 + 3)
                nc.vector.tensor_copy(s2[:, bass.ds(blk * SUB, SUB)], ps[4][:, 0:SUB]).then_inc(scored_d[k], 1)

            def split_x(c):
                w = slice(c * BLOCK, (c + 1) * BLOCK)
                dve.wait_ge(split_h, 2 * c + 1)
                nc.vector.tensor_tensor(x_rest[:, w], xn[:, w], x_head[:, w].bitcast(F32), ALU.subtract).then_inc(split_r, 1)
                dve.wait_ge(split_h, 2 * c + 2)
                nc.vector.tensor_tensor(x2_rest[:, w], grow[:, w], x2_head[:, w].bitcast(F32), ALU.subtract).then_inc(split_r, 1)

            def setup_bias():
                dve.wait_ge(setup_p, 6)
                dve.wait_ge(consts_in, 16 * len(CONSTS))
                nc.vector.tensor_tensor(sqs[:, :], hbias_s[:, :], hbias_s[:, :], ALU.mult).then_inc(setup_d, 1)
                dve.wait_ge(setup_d, 1)
                nc.vector.reduce_sum(bconst[:, 0:1], sqs[:, :], AX.X).then_inc(setup_d, 1)
                dve.wait_ge(setup_d, 2)
                nc.vector.tensor_scalar(bconst[:, 2:3], bconst[:, 0:1], MIN_NORM ** 2, None, ALU.max).then_inc(setup_d, 1)
                nc.vector.tensor_scalar(small[:, 0:2], eps_s[:, :], 2.0, None, ALU.add).then_inc(setup_d, 1)
                dve.wait_ge(setup_d, 4)

            def setup_weights():
                dve.wait_ge(setup_a, 1)
                nc.vector.reciprocal(bconst[:, 2:3], bconst[:, 2:3]).then_inc(setup_d, 1)
                dve.wait_ge(setup_d, 5)
                nc.vector.scalar_tensor_tensor(bconst[:, 1:2], bconst[:, 3:4], MAX_NORM, bconst[:, 2:3], ALU.min, ALU.mult).then_inc(setup_d, 1)
                dve.wait_ge(setup_d, 6)
                nc.vector.scalar_tensor_tensor(bconst[:, 2:3], bconst[:, 1:2], bconst[:, 0:1], bconst[:, 1:2], ALU.mult, ALU.mult).then_inc(setup_d, 1)
                for l in range(2):
                    nc.vector.tensor_tensor(gwd[:, l, 0:D], gw_s[:, l * D:(l + 1) * D], glast_s[:, l * D:(l + 1) * D], ALU.subtract).then_inc(setup_d, 1)
                    nc.vector.tensor_copy(gwd[:, l, D:D + 1], ident[:, P - 1:P]).then_inc(setup_d, 1)
                dve.wait_ge(setup_pe, 1)
                nc.vector.tensor_copy(wa[:, :, :].rearrange("p a b -> p (a b)"), ps[7][:, 0:4]).then_inc(setup_d, 1)
                nc.vector.tensor_copy(hwt_s[:, D:D + 1], ps[7][:, 4:5]).then_inc(setup_d, 1)
                dve.wait_ge(setup_d, 13)
                for l in range(2):
                    nc.vector.tensor_scalar(wa1[:, l, :], ones[:, :], wa[:, l, 0:1], None, ALU.mult).then_inc(setup_d, 1)
                dve.wait_ge(setup_d, SETUP_D)

            ch0 = Chain(dve, chain_d[0], 9)

            def epilogue0(blk, step):
                if step == 2:
                    for h in range(2):
                        if h == 0:
                            dve.wait_ge(bank_done[0], blk * 3 + 3)
                        else:
                            dve.wait_ge(multiplied[0], (blk + 1) * TILES)
                        nc.vector.tensor_scalar(hT[:, 1, h * HALF:(h + 1) * HALF], ps[2 + h][:, :], small[:, 1:2], None,
                                                ALU.mult).then_inc(evac_d[0], 1)
                if 4 <= step < 10:
                    l, h = divmod(step - 4, 2)
                    dve.wait_ge(mlp_mm, blk * 12 + 2 * (step - 4) + 2)
                    nc.vector.tensor_scalar(hT[:, 1, h * HALF:(h + 1) * HALF], ps[6 + h][:, :], bmlp_s[:, 3 + l:4 + l],
                                            0.0, ALU.add, ALU.max).then_inc(evac_d[0], 1)
                if step == 11:
                    dve.wait_ge(bm_added, 1)
                if 11 <= step < 15:
                    b = step - 11
                    dve.wait_ge(natural[0], blk * 4 + b + 1)
                    ch0.step(nc.vector.tensor_tensor(rows[:, b * 256:(b + 1) * 256], ps[4 + b][:, 0:256], col(xn, blk, 2 * b, 2), ALU.add))
                    row_stats(ch0, (2 * b, 2 * b + 1))
                if step == 15:
                    deviation(0, ch0)
                if step == 16:
                    normalise(0, blk)
                if step == 17:
                    keep_rows(0, blk)
                if step == 20:
                    keep_s2(0, blk)

            def stream0(blk, jt):
                if isinstance(blk, int) and jt % SUB == 0:
                    split_x(jt // SUB)
                rest_of(0, blk, jt)
                if isinstance(blk, int) and jt == SUB:
                    setup_bias()
                if isinstance(blk, int) and jt == 3 * SUB:
                    setup_weights()

            pipelined(dve, stream0, epilogue0, ch0)

            def attention_top(k):
                dve.wait_ge(scored_d[k - 1], BLOCKS)
                dve.wait_ge(x_kept[k - 1], BLOCKS)
                nc.vector.reduce_max(small[:, 2:3], s2[:, :], AX.X).then_inc(top_d[k], 1)
                dve.wait_ge(top_pe[k], 1)
                nc.vector.reduce_max(small[0:1, 3:4], ps[4][0:1, 0:P], AX.X).then_inc(top_d[k], 1)
                dve.wait_ge(top_pe[k], 2)
                ch = Chain(dve, chain_d[3 + k])
                nc.vector.tensor_copy(small[:, 4:5], ps[5][:, 0:1])
                nc.vector.tensor_scalar(small[:, 6:7], ps[5][:, 0:1], -0.2, None, ALU.mult)
                ch.step(nc.vector.tensor_scalar(small[:, 5:6], ps[5][:, 0:1], -0.8, None, ALU.mult))
                nc.vector.memset(small[:, 14:15], 0.0).then_inc(top_d[k], 1)
                dve.wait_ge(scored_a[k - 1], 2 * BLOCKS)
                shift_s1(k, 0)
                dve.wait_ge(top_a[k], 1)
                weigh_rows(k, 0)
                dve.wait_ge(top_a[k], 2)
                dve.wait_ge(g_ready[k], 1)

            def shift_s1(k, b):
                nc.vector.tensor_scalar(grow[:, b * BLOCK:(b + 1) * BLOCK], grow[:, b * BLOCK:(b + 1) * BLOCK],
                                        small[:, 4:5], 0.0, ALU.add, ALU.max).then_inc(top_d[k], 1)

            def weigh_rows(k, b):
                xv = xn[:, b * BLOCK:(b + 1) * BLOCK].rearrange("p (t d) -> p t d", d=D)
                xo = xf[:, b * BLOCK:(b + 1) * BLOCK].rearrange("p (t d) -> p t d", d=D)
                fv = Fj[:, b * SUB:(b + 1) * SUB].unsqueeze(2)
                nc.vector.tensor_tensor(xo[:, :, 0:D - 1], xv[:, :, 0:D - 1], fv.broadcast_to([P, SUB, D - 1]), ALU.mult)
                nc.vector.tensor_copy(xo[:, :, D - 1:D], fv).then_inc(xf_ready[k], 1)

            def attention_stream(k, blk, jt):
                if not isinstance(blk, int) and jt == 0:
                    dve.wait_ge(g_ready[k], BLOCKS)
                weigh(k, blk, jt)
                if isinstance(blk, int) and jt in (2, 4, 6):
                    shift_s1(k, jt // 2)
                if isinstance(blk, int) and jt % SUB == 3 and jt < TILES - SUB:
                    weigh_rows(k, jt // SUB + 1)
                if isinstance(blk, int) and k == 1 and jt == SUB:
                    nc.vector.reduce_sum(small[:, 7:8], xsum[:, :], AX.X).then_inc(mean_d, 1)
                    dve.wait_ge(mean_d, 1)
                    nc.vector.tensor_scalar(sqs[:, :], ones[:, :], small[:, 7:8], 1.0 / N, ALU.mult, ALU.mult).then_inc(mean_d, 1)
                if isinstance(blk, int) and k == 1 and jt == 2 * SUB:
                    dve.wait_ge(mean_pe, 1)
                    nc.vector.tensor_copy(meanwh[:, :], ps[6][:, 0:D]).then_inc(mean_d, 1)

            def denominators(k, blk, done, ch):
                for b in range(3):
                    n = min(3, SUB - 3 * b)
                    dve.wait_ge(natural[k], blk * 3 + b + 1)
                    src = ps[4 + b][:, 0:390].rearrange("p (t c) -> p t c", c=130)[:, 0:n, D]
                    last = nc.vector.tensor_copy(den[:, 3 * b:3 * b + n], src)
                ch.step(last)
                ch.step(nc.vector.tensor_scalar(zero[:, :], den[:, :], 0.0, None, ALU.is_equal))
                ch.step(nc.vector.tensor_tensor(den[:, :], den[:, :], zero[:, :], ALU.add))
                nc.vector.reciprocal(rden[:, :], den[:, :]).then_inc(done, 1)
                dve.wait_ge(done, blk + 1)

            def nat(it):
                return ps[4 + it // 3][:, (it % 3) * 130:(it % 3) * 130 + D]

            attention_top(1)
            ch1 = Chain(dve, chain_d[1], 12)

            def epilogue1(blk, step):
                if step == 4:
                    denominators(1, blk, rden_ready, ch1)
                if step in (6, 7):
                    for it in range(4 * (step - 6), 4 * (step - 5)):
                        dve.wait_ge(scaled, blk * SUB + it + 1)
                        last = nc.vector.scalar_tensor_tensor(rows[:, it * P:(it + 1) * P], meanwh[:, :], zero[:, it:it + 1],
                                                              rows[:, it * P:(it + 1) * P], ALU.mult, ALU.add)
                    ch1.step(last)
                if step == 8:
                    nc.vector.tensor_scalar(tmp[:, :], rows[:, :], 0.0, None, ALU.min).then_inc(elu_d, 1)
                if step == 9:
                    ch1.step(nc.vector.scalar_tensor_tensor(rows[:, :], rows[:, :], 0.0, col(xn, blk, 0, SUB), ALU.max, ALU.add))
                if step == 11:
                    dve.wait_ge(elu_a, blk + 1)
                    ch1.step(nc.vector.scalar_tensor_tensor(rows[:, :], tmp[:, :], -1.0, rows[:, :], ALU.add, ALU.add))
                if 12 <= step < 16:
                    row_stats(ch1, (2 * step - 24, 2 * step - 23))
                if step == 16:
                    deviation(1, ch1)
                if step == 18:
                    norm_bias(1, blk)
                if step == 26:
                    keep_s2(1, blk)

            pipelined(dve, lambda blk, jt: attention_stream(1, blk, jt), epilogue1, ch1)

            attention_top(2)
            ch2 = Chain(dve, chain_d[2], 40)

            def artanh_ln(ch, t):
                ch.step(nc.vector.tensor_scalar(sc[:, 10, :], sc[:, t, :], -1.0, 1.0, ALU.mult, ALU.add))
                ch.step(nc.vector.reciprocal(sc[:, 10, :], sc[:, 10, :]))
                ch.step(nc.vector.scalar_tensor_tensor(sc[:, 7, :], sc[:, t, :], 2.0, sc[:, 10, :], ALU.mult, ALU.mult))
                nc.vector.tensor_scalar(sc[:, 8, :], sc[:, 7, :], 1.0, None, ALU.add).then_inc(hyp_d, 1)

            def artanh_rest(ch, o, asked, ln):
                dve.wait_ge(hyp_d, asked)
                ch.step(nc.vector.tensor_scalar(sc[:, 10, :], sc[:, 8, :], -1.0, None, ALU.add))
                ch.step(nc.vector.tensor_scalar(sc[:, 11, :], sc[:, 10, :], 0.0, None, ALU.is_equal))
                ch.step(nc.vector.tensor_tensor(sc[:, 10, :], sc[:, 10, :], sc[:, 11, :], ALU.add))
                ch.step(nc.vector.reciprocal(sc[:, 10, :], sc[:, 10, :]))
                dve.wait_ge(hyp_a, ln)
                ch.step(nc.vector.tensor_tensor(sc[:, 9, :], sc[:, 9, :], sc[:, 11, :], ALU.add))
                ch.step(nc.vector.tensor_tensor(sc[:, 9, :], sc[:, 9, :], sc[:, 10, :], ALU.mult))
                ch.step(nc.vector.scalar_tensor_tensor(sc[:, o, :], sc[:, 7, :], 0.5, sc[:, 9, :], ALU.mult, ALU.mult))

            def epilogue2(blk, step):
                if step == 3:
                    denominators(2, blk, rden_ready2, ch2)
                if 4 <= step < 8:
                    for it in (2 * step - 8, 2 * step - 7):
                        last = nc.vector.scalar_tensor_tensor(rows[:, it * P:(it + 1) * P], nat(it), rden[:, it:it + 1],
                                                              col(xn, blk, it), ALU.mult, ALU.add)
                    last.then_inc(rows_done, 1)
                if 5 <= step < 9:
                    dve.wait_ge(rows_done, blk * 4 + step - 4)
                    row_stats(ch2, (2 * step - 10, 2 * step - 9))
                if step == 9:
                    deviation(2, ch2)
                if step == 11:
                    norm_bias(2, blk)
                    ch2.step(nc.vector.tensor_tensor(sc[:, 19, :], rstd[:, :], rstd[:, :], ALU.mult))
                    ch2.mark(nc.vector.scalar_tensor_tensor(sc[:, 0, :], mv[:, :, 1], float(D), sc[:, 19, :], ALU.mult, ALU.mult))
                if step == 18:
                    ch2.wait()
                    dve.wait_ge(hyp_a, blk * 6 + 1)
                    nc.vector.tensor_scalar(sc[:, 3:5, :], sc[:, 0:2, :], MIN_NORM ** 2, None, ALU.max).then_inc(root_asked[2], 1)
                if step == 20:
                    dve.wait_ge(root_done[2], blk * 3 + 2)
                    nc.vector.reciprocal(sc[:, 12, :], sc[:, 3, :])
                    nc.vector.reciprocal(sc[:, 13, :], sc[:, 4, :])
                    ch2.step(nc.vector.tensor_scalar(sc[:, 14, :], sc[:, 3, :], CLIP, None, ALU.min))
                    artanh_ln(ch2, 14)
                if step == 21:
                    artanh_rest(ch2, 15, blk * 6 + 1, blk * 6 + 2)
                    ch2.step(nc.vector.tensor_tensor(sc[:, 12, :], sc[:, 4, :], sc[:, 12, :], ALU.mult))
                    nc.vector.tensor_tensor(sc[:, 5, :], sc[:, 12, :], sc[:, 15, :], ALU.mult).then_inc(hyp_d, 1)
                if step == 22:
                    dve.wait_ge(hyp_a, blk * 6 + 3)
                    ch2.step(nc.vector.scalar_tensor_tensor(sc[:, 6, :], sc[:, 6, :], MAX_NORM, sc[:, 13, :], ALU.min, ALU.mult))
                    ch2.step(nc.vector.tensor_tensor(sc[:, 12, :], sc[:, 6, :], sc[:, 6, :], ALU.mult))
                    nc.vector.tensor_tensor(sc[:, 12, :], sc[:, 12, :], sc[:, 1, :], ALU.mult)
                    ch2.step(nc.vector.scalar_tensor_tensor(sc[:, 13, :], sc[:, 2, :], bconst[:, 1:2], sc[:, 6, :], ALU.mult, ALU.mult))
                    ch2.step(nc.vector.tensor_scalar(sc[:, 14, :], sc[:, 13, :], 2.0, 1.0, ALU.mult, ALU.add))
                    nc.vector.scalar_tensor_tensor(sc[:, 15, :], sc[:, 14, :], bconst[:, 2:3], sc[:, 6, :], ALU.add, ALU.mult)
                    nc.vector.tensor_scalar(sc[:, 17, :], sc[:, 12, :], -1.0, 1.0, ALU.mult, ALU.add)
                    ch2.step(nc.vector.scalar_tensor_tensor(sc[:, 18, :], sc[:, 12, :], bconst[:, 2:3], sc[:, 14, :], ALU.mult, ALU.add))
                    ch2.step(nc.vector.tensor_scalar(sc[:, 18, :], sc[:, 18, :], MIN_NORM, None, ALU.max))
                    ch2.step(nc.vector.reciprocal(sc[:, 18, :], sc[:, 18, :]))
                    nc.vector.tensor_tensor(sc[:, 15, :], sc[:, 15, :], sc[:, 18, :], ALU.mult)
                    nc.vector.scalar_tensor_tensor(sc[:, 17, :], sc[:, 17, :], bconst[:, 1:2], sc[:, 18, :], ALU.mult, ALU.mult).then_inc(hyp_d, 1)
                if step == 23:
                    dve.wait_ge(hyp_d, blk * 6 + 3)
                    dve.wait_ge(hyp_a, blk * 6 + 4)
                if step in (23, 24):
                    for it in range(4 * (step - 23), 4 * (step - 22)):
                        t = tmp[:, it * P:(it + 1) * P]
                        last = nc.vector.scalar_tensor_tensor(t, t, sc[:, 15, it:it + 1], rows[:, it * P:(it + 1) * P], ALU.mult, ALU.add)
                if step == 24:
                    last.then_inc(hyp_d, 1)
                if step == 26:
                    dve.wait_ge(hyp_a, blk * 6 + 5)
                    nc.vector.tensor_scalar(sc[:, 3, :], sc[:, 0, :], MIN_NORM ** 2, None, ALU.max).then_inc(root_asked[2], 1)
                if step == 28:
                    dve.wait_ge(root_done[2], blk * 3 + 3)
                    nc.vector.reciprocal(sc[:, 12, :], sc[:, 3, :])
                    ch2.step(nc.vector.tensor_scalar(sc[:, 14, :], sc[:, 3, :], MAX_NORM, None, ALU.min))
                    artanh_ln(ch2, 14)
                if step == 29:
                    artanh_rest(ch2, 15, blk * 6 + 5, blk * 6 + 6)
                    nc.vector.tensor_tensor(sc[:, 16, :], sc[:, 15, :], sc[:, 12, :], ALU.mult).then_inc(hyp_d, 1)
                if step == 31:
                    dve.wait_ge(hyp_d, blk * 6 + 6)
                    for it in range(SUB):
                        if it % 4 == 0:
                            dve.wait_ge(hyp_out_a, blk * 2 + it // 4 + 1)
                        last = nc.vector.scalar_tensor_tensor(col(x_rest, blk, it), tmp[:, it * P:(it + 1) * P], sc[:, 16, it:it + 1],
                                                              col(x_head, blk, it).bitcast(F32), ALU.mult, ALU.subtract)
                    last.then_inc(hyp_out_d, 1)

            pipelined(dve, lambda blk, jt: attention_stream(2, blk, jt), epilogue2, ch2, tail=False)

            ch3 = Chain(dve, chain_d[3], 11)

            def epilogue3(blk, step):
                if step == 5 and isinstance(blk, int):
                    dve.wait_ge(rows_read, blk * 2 + 2)
                    nc.vector.tensor_scalar(tmp[:, :], rows[:, :], 0.0, None, ALU.max).then_inc(relu_done, 1)
                if step == 12:
                    dve.wait_ge(fin_a, blk * 3 + 2)
                    nc.vector.tensor_scalar(sc[:, 0:2, :], sc[:, 0:2, :], MIN_NORM ** 2, None, ALU.max).then_inc(root_asked[3], 1)
                if step == 15:
                    dve.wait_ge(root_done[3], blk * 2 + 1)
                    ch3.step(nc.vector.reciprocal(sc[:, 3, :], sc[:, 0, :]))
                    ch3.step(nc.vector.scalar_tensor_tensor(sc[:, 2, :], sc[:, 0, :], ATANH_MAX, sc[:, 3, :], ALU.min, ALU.mult))
                    ch3.step(nc.vector.tensor_tensor(sc[:, 4, :], sc[:, 1, :], sc[:, 2, :], ALU.mult))
                    nc.vector.tensor_scalar(sc[:, 4, :], sc[:, 4, :], MIN_NORM, None, ALU.max).then_inc(fin_d, 1)
                if step == 18:
                    dve.wait_ge(fin_d, blk + 1)
                    ch3.step(nc.vector.reciprocal(sc[:, 6, :], sc[:, 4, :]))
                    dve.wait_ge(fin_a, blk * 3 + 3)
                    ch3.step(nc.vector.scalar_tensor_tensor(sc[:, 5, :], sc[:, 5, :], MAX_NORM, sc[:, 6, :], ALU.min, ALU.mult))
                    ch3.step(nc.vector.tensor_tensor(sc[:, 5, :], sc[:, 5, :], sc[:, 2, :], ALU.mult))
                if 19 <= step < 23:
                    for it in (2 * step - 38, 2 * step - 37):
                        last = nc.vector.scalar_tensor_tensor(rows[:, it * P:(it + 1) * P], tmp[:, it * P:(it + 1) * P], sc[:, 5, it:it + 1],
                                                              col(xn, blk, it), ALU.mult, ALU.add)
                    last.then_inc(final_rows, 1)
                if 20 <= step < 24:
                    dve.wait_ge(final_rows, blk * 4 + step - 19)
                    row_stats(ch3, (2 * step - 40, 2 * step - 39))
                if step == 24:
                    deviation(3, ch3)
                if step == 26:
                    norm_bias(3, blk)

            pipelined(dve, lambda blk, jt: rest_of(3, blk, jt), epilogue3, ch3,
                      before=lambda step: epilogue2(BLOCKS - 1, step))

        @block.tensor
        def _(pe):
            def weight_setup():
                pe.wait_ge(consts_in, 16 * len(CONSTS))
                for l in range(2):
                    nc.tensor.matmul(ps[7][:, 2 * l:2 * l + 2], gwt_s[:, l * D:(l + 1) * D], ga_s[:, 2 * l:2 * l + 2], start=True, stop=True)
                nc.tensor.matmul(ps[7][:, 4:5], hw_s[:, :], hbcol_s[:, :], start=True, stop=True).then_inc(setup_pe, 1)

            def split_products(k, blk, jt, operands):
                r = jt % RING
                j = slice(jt * P, (jt + 1) * P)
                pe.wait_ge(heads[k], blk * TILES + jt + 1)
                if jt == TILES - 1 or jt == 0 and not isinstance(blk, int):
                    wait_rest(k, blk, jt)
                    for n, (xh, xr) in enumerate(operands):
                        for h in range(2):
                            if jt == 0 and not isinstance(blk, int):
                                if k == 0:
                                    pe.wait_ge((evac_a, evac_d)[n][0], blk * 8 - 7 + h)
                                else:
                                    pe.wait_ge(evac_a[k], blk * 2 - 1 + h)
                            bank, cols = ps[2 * n + h][:, :], slice(h * HALF, (h + 1) * HALF)
                            nc.tensor.matmul(bank, xh[:, j], head[:, r, cols], start=(jt == 0), stop=False)
                            nc.tensor.matmul(bank, xr[:, j], head[:, r, cols], start=False, stop=False)
                            last = nc.tensor.matmul(bank, xh[:, j], rest[:, r, cols], start=False, stop=(jt == TILES - 1))
                            if jt == TILES - 1 and 2 * n + h < 2 * len(operands) - 1:
                                last.then_inc(bank_done[k], 1)
                    last.then_inc(multiplied[k], 1)
                    return
                for n, (xh, xr) in enumerate(operands):
                    for w in (xh, xr):
                        for h in range(2):
                            nc.tensor.matmul(ps[2 * n + h][:, :], w[:, j], head[:, r, h * HALF:(h + 1) * HALF],
                                             start=(jt == 0 and w is xh), stop=False)
                wait_rest(k, blk, jt)
                for n, (xh, xr) in enumerate(operands):
                    for h in range(2):
                        last = nc.tensor.matmul(ps[2 * n + h][:, :], xh[:, j], rest[:, r, h * HALF:(h + 1) * HALF],
                                                start=False, stop=False)
                last.then_inc(multiplied[k], 1)

            def wait_rest(k, blk, jt):
                if k == 3 and not isinstance(blk, int):
                    by_pool = len([t for t in POOL_RESTS if t <= jt])
                    if jt in POOL_RESTS:
                        pe.wait_ge(pool_rests, (blk - 1) * len(POOL_RESTS) + by_pool)
                    else:
                        pe.wait_ge(rests[k], TILES + (blk - 1) * (TILES - len(POOL_RESTS)) + jt + 1 - by_pool)
                else:
                    pe.wait_ge(rests[k], blk * TILES + jt + 1)

            def turn(k, blk):
                for h in range(2):
                    pe.wait_ge(x_ready[k], blk * 2 + h + 1)
                    for q in range(4):
                        last = nc.tensor.transpose(ps[4 + h][:, q * P:(q + 1) * P], rows[:, (4 * h + q) * P:(4 * h + q + 1) * P], ident[:, :])
                    last.then_inc(turned[k], 1)

            def score(k, blk):
                l = k
                for h in range(2):
                    pe.wait_ge(xT_ready[k], blk * 2 + h + 1)
                    nc.tensor.matmul(ps[6 + h][:, :], wa1[:, l, :], xT[:, h * HALF:(h + 1) * HALF],
                                     start=True, stop=True).then_inc(scores[k], 1)
                for it in range(SUB):
                    last = nc.tensor.matmul(ps[4][:, it:it + 1], xT[:, it * P:(it + 1) * P], wa[:, l, 1:2], start=True, stop=True)
                last.then_inc(scores[k], 1)

            def stream0(blk, jt):
                if isinstance(blk, int) and jt % SUB == 0:
                    pe.wait_ge(split_h, jt // SUB * 2 + 2)
                    pe.wait_ge(split_r, jt // SUB * 2 + 2)
                split_products(0, blk, jt, ((x_head, x_rest), (x2_head, x2_rest)))
                if isinstance(blk, int) and jt == SUB:
                    weight_setup()

            def epilogue0(blk, step):
                if 1 <= step < 7:
                    l, h = divmod(step - 1, 2)
                    for n, evac in ((0, evac_a), (1, evac_d)):
                        pe.wait_ge(evac[0], blk * 8 + 2 * l + h + 1)
                        w = (3 * n + l) * D
                        nc.tensor.matmul(ps[4 + 2 * n + h][:, :], wmlp_s[:, w:w + D], hT[:, n, h * HALF:(h + 1) * HALF],
                                         start=True, stop=True).then_inc(mlp_mm, 1)
                if 8 <= step < 12:
                    b = step - 8
                    pe.wait_ge(evac_a[0], blk * 8 + 8)
                    pe.wait_ge(evac_d[0], blk * 8 + 8)
                    for it in (2 * b, 2 * b + 1):
                        for n in range(2):
                            last = nc.tensor.matmul(ps[4 + b][:, (it % 2) * P:(it % 2 + 1) * P], hT[:, n, it * P:(it + 1) * P],
                                                    wmlp_s[:, (6 + n) * D:(7 + n) * D], start=(n == 0), stop=(n == 1))
                    last.then_inc(natural[0], 1)
                if step == 15:
                    turn(0, blk)
                if step == 17:
                    pe.wait_ge(setup_d, SETUP_D)
                    score(0, blk)

            pipelined(pe, stream0, epilogue0)

            def attention_top(k):
                pe.wait_ge(top_d[k], 1)
                pe.wait_ge(scored_a[k - 1], 2 * BLOCKS)
                nc.tensor.transpose(ps[4][0:1, 0:P], small[:, 2:3], ident[:, :]).then_inc(top_pe[k], 1)
                pe.wait_ge(top_d[k], 2)
                nc.tensor.matmul(ps[5][:, 0:1], ones[0:1, :], small[0:1, 3:4], start=True, stop=True).then_inc(top_pe[k], 1)

            def attention_stream(k, blk, jt):
                if isinstance(blk, int) and jt % SUB == 0:
                    pe.wait_ge(xf_ready[k], jt // SUB + 1)
                pe.wait_ge(used[k], blk * TILES + jt + 1)
                for h in range(2):
                    if jt == 0 and not isinstance(blk, int):
                        pe.wait_ge(evac_a[k], blk * 2 - 1 + h)
                    last = nc.tensor.matmul(ps[h][:, :], xf[:, jt * P:(jt + 1) * P], ring[:, jt % RING, h * HALF:(h + 1) * HALF],
                                            start=(jt == 0), stop=(jt == TILES - 1))
                    if jt == TILES - 1 and h == 0:
                        last.then_inc(bank_done[k], 1)
                last.then_inc(multiplied[k], 1)
                if isinstance(blk, int) and k == 1 and jt == SUB + RING:
                    pe.wait_ge(mean_d, 2)
                    nc.tensor.matmul(ps[6][:, 0:D], sqs[:, :], gw_s[:, 0:D], start=True, stop=True).then_inc(mean_pe, 1)
                if isinstance(blk, int) and k == 1 and jt == TILES - 1:
                    pe.wait_ge(mean_d, 3)

            def attention_rows(k, blk):
                pe.wait_ge(evac_a[k], blk * 2 + 2)
                for it in range(SUB):
                    last = nc.tensor.matmul(ps[4 + it // 3][:, (it % 3) * 130:(it % 3) * 130 + D + 1], hT[:, 0, it * P:(it + 1) * P],
                                            gwd[:, k - 1, :], start=True, stop=True)
                    if it % 3 == 2 or it == SUB - 1:
                        last.then_inc(natural[k], 1)

            attention_top(1)

            def epilogue1(blk, step):
                if step == 0:
                    attention_rows(1, blk)
                if step == 18:
                    turn(1, blk)
                if step == 21:
                    score(1, blk)

            pipelined(pe, lambda blk, jt: attention_stream(1, blk, jt), epilogue1)

            attention_top(2)

            def epilogue2(blk, step):
                if step == 0:
                    attention_rows(2, blk)
                if step == 11:
                    turn(2, blk)
                if step == 13:
                    pe.wait_ge(xT_ready[2], blk * 2 + 2)
                    for it in range(SUB):
                        last = nc.tensor.matmul(ps[4 + it // 3][:, (it % 3) * 130:(it % 3) * 130 + D + 1], xT[:, it * P:(it + 1) * P],
                                                hwt_s[:, :], start=True, stop=True)
                        if it % 3 == 2 or it == SUB - 1:
                            last.then_inc(scores[2], 1)

            pipelined(pe, lambda blk, jt: attention_stream(2, blk, jt), epilogue2, tail=False)

            def stream3(blk, jt):
                if isinstance(blk, int):
                    if jt == 0:
                        pe.wait_ge(evac_a[2], BLOCKS * 2)
                    if jt % SUB == 0:
                        pe.wait_ge(hyp_out_d, jt // SUB + 1)
                        pe.wait_ge(hyp_out_a, 2 * (jt // SUB + 1))
                split_products(3, blk, jt, ((x_head, x_rest),))

            def epilogue3(blk, step):
                if step == 1:
                    pe.wait_ge(evac_a[3], blk * 2 + 2)
                    for h in range(2):
                        for q in range(4):
                            it = 4 * h + q
                            last = nc.tensor.transpose(ps[4 + h][:, q * P:(q + 1) * P], hT[:, 0, it * P:(it + 1) * P], ident[:, :])
                        last.then_inc(natural[3], 1)

            pipelined(pe, stream3, epilogue3, before=lambda step: epilogue2(BLOCKS - 1, step))


def kernel(**inputs):
    import numpy as np
    import concourse.bacc as bacc
    from concourse.bass_utils import run_bass_kernel_spmd

    a = {k: np.asarray(v) for k, v in inputs.items()}

    def rows(v):
        return np.ascontiguousarray(v.reshape(TILES, P, D).transpose(1, 0, 2).reshape(P, N))

    def everywhere(v):
        return np.ascontiguousarray(np.broadcast_to(v.reshape(1, -1), (P, v.size)))

    W1, W2, Wm = a["L0_gnn_W1"], a["L0_gnn_W2"], a["L0_gnn_Wm"]
    gW = [a["L1_gnn_W"], a["L2_gnn_W"]]
    ga = [a["L1_gnn_a"].reshape(2, D), a["L2_gnn_a"].reshape(2, D)]
    arrays = {
        "adj": np.ascontiguousarray(a["adj"].reshape(BLOCKS, BLOCK, TILES, P).transpose(0, 2, 3, 1)).reshape(STREAM * P, BLOCK),
        "x": rows(a["x"]),
        "x2": rows(a["L0_gnn_x2"]),
        "wmlp": np.ascontiguousarray(np.concatenate([w.T for w in W1] + [w.T for w in W2] + [Wm[:, :D].T, Wm[:, D:].T], axis=1)),
        "bmlp": np.ascontiguousarray(np.concatenate([a["L0_gnn_b1"], a["L0_gnn_b2"]]).T),
        "eps": everywhere(np.concatenate([a["L0_gnn_eps1"], a["L0_gnn_eps2"]])),
        "bm": everywhere(a["L0_gnn_bm"]),
        "gw": np.ascontiguousarray(np.concatenate(gW, axis=1)),
        "gwt": np.ascontiguousarray(np.concatenate([w.T for w in gW], axis=1)),
        "glast": np.concatenate([everywhere(w[-1]) for w in gW], axis=1),
        "ga": np.ascontiguousarray(np.concatenate(ga).T),
        "hwt": np.ascontiguousarray(a["L3_gnn_weight"].T),
        "hw": np.ascontiguousarray(a["L3_gnn_weight"]),
        "hbias": everywhere(a["L3_gnn_bias"]),
        "hbcol": a["L3_gnn_bias"].reshape(D, 1),
        "ident": np.eye(P, dtype=np.float32),
    }
    nc = bacc.Bacc("TRN2", target_bir_lowering=False, num_devices=1)
    feed, args = {}, []
    for name, v in arrays.items():
        feed[f"in_{name}"] = v
        args.append(nc.dram_tensor(f"in_{name}", v.shape, mybir.dt.from_np(v.dtype), kind="ExternalInput").ap())
    args.append(nc.dram_tensor("out_rows", (P, N), F32, kind="ExternalOutput").ap())
    build(nc, *args)
    r = run_bass_kernel_spmd(nc, [feed], core_ids=[0])
    got = r.results[0]["out_rows"]
    return np.ascontiguousarray(got.reshape(P, TILES, D).transpose(1, 0, 2)).reshape(N, D)
```
